# Optimizing a Trainium2 kernel written in Bass

```python
import numpy as np
import jax
import jax.numpy as jnp

def _softmax(x, axis=-1):
    return jax.nn.softmax(x, axis=axis)

def _gelu(x):
    return jax.nn.gelu(x, approximate=True)

def _silu(x):
    return jax.nn.silu(x)

def _sigmoid(x):
    return jax.nn.sigmoid(x)

def _layernorm(x, axis=-1, eps=1e-05):
    m = jnp.mean(x, axis=axis, keepdims=True)
    v = jnp.var(x, axis=axis, keepdims=True)
    return (x - m) / jnp.sqrt(v + eps)

def _scatter_add(tgt, idx, src, axis=0):
    return tgt.at[idx].add(src)

def _segment_sum(src, seg, n):
    return jax.ops.segment_sum(src, seg, n)
kernel_name = 'mk_adaln_attn_ffn_d1_seqx_r4_01c8d5'

def setup_inputs(seed: int=0):
    np.random.seed(seed)
    _w = jnp.asarray

    def _rec_inputs():
        import jax
        import jax.numpy as jnp
        _rk = jax.random.key(seed)
        x = -0.000125 + 0.9999 * jax.random.normal(jax.random.fold_in(_rk, 1), (32, 64, 1024), jnp.float32)
        _lenS = 64 - jax.random.randint(jax.random.fold_in(_rk, 7), (32,), 0, max(1, 64 // 4) + 1, jnp.int32)
        _lenS2 = 64 - jax.random.randint(jax.random.fold_in(_rk, 8), (32,), 0, max(1, 64 // 4) + 1, jnp.int32)
        cond_128 = 0.0061147 + 1.02565 * jax.random.normal(jax.random.fold_in(_rk, 11), (32, 128), jnp.float32)
        fside_S_0 = -0.022604 + 0.987366 * jax.random.normal(jax.random.fold_in(_rk, 12), (64,), jnp.float32)
        return (x, cond_128, fside_S_0)
    x, cond_128, fside_S_0 = _rec_inputs()

    def _L0_cond_setup():
        import jax, jax.numpy as jnp
        import numpy as np
        K = 8
        T = 1.0
        D_EMBD = 128
        IN_C = 64
        OUT_C = 64
        BS = 32
        H = 1024
        HID = 128
        key = jax.random.key(seed)
        ks = jax.random.split(key, 10)
        s = lambda fan_in: 1.0 / np.sqrt(fan_in)
        return {'x': jax.random.normal(ks[0], (BS, IN_C, H), dtype=jnp.float32), 'embedding': jax.random.normal(ks[1], (BS, D_EMBD), dtype=jnp.float32), 'W0': jax.random.normal(ks[2], (D_EMBD, HID), dtype=jnp.float32) * s(D_EMBD), 'b0': jnp.zeros((HID,), dtype=jnp.float32), 'W1': jax.random.normal(ks[3], (HID, HID), dtype=jnp.float32) * s(HID), 'b1': jnp.zeros((HID,), dtype=jnp.float32), 'W2': jax.random.normal(ks[4], (HID, K), dtype=jnp.float32) * s(HID), 'b2': jnp.zeros((K,), dtype=jnp.float32), 'weight': jax.random.normal(ks[5], (K, OUT_C, IN_C, 1), dtype=jnp.float32) * s(IN_C), 'bias_k': jax.random.normal(ks[6], (K, OUT_C), dtype=jnp.float32) * 0.1}
    _L0_cond_all = _L0_cond_setup()
    _L0_cond_in = {k: v for k, v in _L0_cond_all.items() if k in ('W0', 'b0', 'W1', 'b1', 'W2', 'b2', 'weight', 'bias_k')}
    del _L0_cond_all

    def _L0_attn_setup():
        import jax, jax.numpy as jnp
        import numpy as np
        NEG_INF = -1e+30

        def rotary_pos_emb(x):
            B, T, H, D = x.shape
            exponents = (jnp.arange(0, D, 2)[:D // 2] // D).astype(jnp.float32)
            freqs = 1.0 / jnp.power(jnp.float32(1000.0), exponents)
            theta = jnp.arange(T, dtype=jnp.float32)[:, None] * freqs[None, :]
            cos = jnp.cos(theta)[None, :, None, :]
            sin = jnp.sin(theta)[None, :, None, :]
            xr = x.astype(jnp.float32).reshape(B, T, H, D // 2, 2)
            x0, x1 = (xr[..., 0], xr[..., 1])
            out = jnp.stack([x0 * cos - x1 * sin, x0 * sin + x1 * cos], axis=-1)
            return out.reshape(B, T, H, D).astype(x.dtype)

        def attention_fwd(x, wq, wk, wv, wo, n_heads=32):
            B, T, C = x.shape
            hd = C // n_heads
            xq = (x @ wq.T).reshape(B, T, n_heads, hd)
            xk = (x @ wk.T).reshape(B, T, n_heads, hd)
            xv = (x @ wv.T).reshape(B, T, n_heads, hd)
            xq = rotary_pos_emb(xq)
            xk = rotary_pos_emb(xk)
            scale = hd ** (-0.5)
            scores = jnp.einsum('bqhd,bkhd->bhqk', xq, xk) * scale
            causal = jnp.tril(jnp.ones((T, T), dtype=bool))
            scores = jnp.where(causal[None, None], scores, NEG_INF)
            probs = jax.nn.softmax(scores.astype(jnp.float32), axis=-1).astype(xq.dtype)
            out = jnp.einsum('bhqk,bkhd->bqhd', probs, xv).reshape(B, T, C)
            return out @ wo.T
        key = jax.random.key(seed)
        ks = jax.random.split(key, 5)
        B, T, C = (2, 512, 1024)
        s = 0.02
        return {'x': jax.random.normal(ks[0], (B, T, C), jnp.float32), 'wq': jax.random.normal(ks[1], (C, C), jnp.float32) * s, 'wk': jax.random.normal(ks[2], (C, C), jnp.float32) * s, 'wv': jax.random.normal(ks[3], (C, C), jnp.float32) * s, 'wo': jax.random.normal(ks[4], (C, C), jnp.float32) * s}
    _L0_attn_all = _L0_attn_setup()
    _L0_attn_in = {k: v for k, v in _L0_attn_all.items() if k in ('wq', 'wk', 'wv', 'wo')}
    del _L0_attn_all

    def _L0_cond2_setup():
        import jax, jax.numpy as jnp
        import numpy as np
        from jax import lax
        N, C_IN, L = (32, 64, 1024)
        C_OUT, K, GROUPS = (64, 9, 4)
        C_DIM, PAD, STRIDE = (128, 4, 1)
        key = jax.random.key(seed)
        k1, k2, k3, k4, k5 = jax.random.split(key, 5)
        x = jax.random.normal(k1, (N, C_IN, L), dtype=jnp.float32)
        c = jax.random.normal(k2, (N, C_DIM), dtype=jnp.float32)
        weight = jax.random.normal(k3, (C_OUT, C_IN // GROUPS, K), dtype=jnp.float32)
        c_weight = jax.random.normal(k4, (C_OUT, C_DIM), dtype=jnp.float32)
        bias = jax.random.normal(k5, (C_OUT,), dtype=jnp.float32)
        return {'x': x, 'c': c, 'weight': weight, 'c_weight': c_weight, 'bias': bias}
    _L0_cond2_all = _L0_cond2_setup()
    _L0_cond2_in = {k: v for k, v in _L0_cond2_all.items() if k in ('weight', 'c_weight')}
    del _L0_cond2_all

    def _L0_ffn_setup():
        import jax, jax.numpy as jnp
        import numpy as np
        ALPHA = 32
        R = 16
        SCALING = ALPHA / R
        key = jax.random.key(seed)
        k1, k2, k3, k4 = jax.random.split(key, 4)
        B_, S, D = (4, 512, 1024)
        H, r, O = (8, R, 1024)
        x = jax.random.normal(k1, (B_, S, D), dtype=jnp.float32)
        A = jax.random.normal(k2, (H, r, D), dtype=jnp.float32) * 0.02
        Bm = jax.random.normal(k3, (H, O, r), dtype=jnp.float32) * 0.02
        Wr = jax.random.normal(k4, (H, D), dtype=jnp.float32) * 0.02
        br = jnp.zeros((H,), dtype=jnp.float32)
        return {'x': x, 'A': A, 'B': Bm, 'Wr': Wr, 'br': br}
    _L0_ffn_all = _L0_ffn_setup()
    _L0_ffn_in = {k: v for k, v in _L0_ffn_all.items() if k in ('A', 'B', 'Wr', 'br')}
    del _L0_ffn_all
    return {'x': x, 'cond_128': cond_128, 'fside_S_0': fside_S_0, 'L0_cond_W0': _L0_cond_in['W0'], 'L0_cond_b0': _L0_cond_in['b0'], 'L0_cond_W1': _L0_cond_in['W1'], 'L0_cond_b1': _L0_cond_in['b1'], 'L0_cond_W2': _L0_cond_in['W2'], 'L0_cond_b2': _L0_cond_in['b2'], 'L0_cond_weight': _L0_cond_in['weight'], 'L0_cond_bias_k': _L0_cond_in['bias_k'], 'L0_attn_wq': _L0_attn_in['wq'], 'L0_attn_wk': _L0_attn_in['wk'], 'L0_attn_wv': _L0_attn_in['wv'], 'L0_attn_wo': _L0_attn_in['wo'], 'L0_cond2_weight': _L0_cond2_in['weight'], 'L0_cond2_c_weight': _L0_cond2_in['c_weight'], 'L0_ffn_A': _L0_ffn_in['A'], 'L0_ffn_B': _L0_ffn_in['B'], 'L0_ffn_Wr': _L0_ffn_in['Wr'], 'L0_ffn_br': _L0_ffn_in['br']}

def reference(x, cond_128, fside_S_0, L0_cond_W0, L0_cond_b0, L0_cond_W1, L0_cond_b1, L0_cond_W2, L0_cond_b2, L0_cond_weight, L0_cond_bias_k, L0_attn_wq, L0_attn_wk, L0_attn_wv, L0_attn_wo, L0_cond2_weight, L0_cond2_c_weight, L0_ffn_A, L0_ffn_B, L0_ffn_Wr, L0_ffn_br):
    import jax
    import jax.numpy as jnp

    def _L0_cond_ref(x, embedding, W0, b0, W1, b1, W2, b2, weight, bias_k):
        import jax, jax.numpy as jnp
        import numpy as np
        K = 8
        T = 1.0
        D_EMBD = 128
        IN_C = 64
        OUT_C = 64
        BS = 32
        H = 1024
        HID = 128
        h = jax.nn.gelu(embedding @ W0 + b0, approximate=False)
        h = jax.nn.gelu(h @ W1 + b1, approximate=False)
        att = jax.nn.softmax((h @ W2 + b2) / T, axis=-1)
        agg_w = jnp.einsum('bk,koi->boi', att, weight[..., 0])
        agg_b = att @ bias_k
        out = jnp.einsum('boi,bih->boh', agg_w, x) + agg_b[:, :, None]
        return out

    def _L0_attn_ref(x, wq, wk, wv, wo):
        import jax, jax.numpy as jnp
        import numpy as np
        NEG_INF = -1e+30

        def rotary_pos_emb(x):
            B, T, H, D = x.shape
            exponents = (jnp.arange(0, D, 2)[:D // 2] // D).astype(jnp.float32)
            freqs = 1.0 / jnp.power(jnp.float32(1000.0), exponents)
            theta = jnp.arange(T, dtype=jnp.float32)[:, None] * freqs[None, :]
            cos = jnp.cos(theta)[None, :, None, :]
            sin = jnp.sin(theta)[None, :, None, :]
            xr = x.astype(jnp.float32).reshape(B, T, H, D // 2, 2)
            x0, x1 = (xr[..., 0], xr[..., 1])
            out = jnp.stack([x0 * cos - x1 * sin, x0 * sin + x1 * cos], axis=-1)
            return out.reshape(B, T, H, D).astype(x.dtype)

        def attention_fwd(x, wq, wk, wv, wo, n_heads=32):
            B, T, C = x.shape
            hd = C // n_heads
            xq = (x @ wq.T).reshape(B, T, n_heads, hd)
            xk = (x @ wk.T).reshape(B, T, n_heads, hd)
            xv = (x @ wv.T).reshape(B, T, n_heads, hd)
            xq = rotary_pos_emb(xq)
            xk = rotary_pos_emb(xk)
            scale = hd ** (-0.5)
            scores = jnp.einsum('bqhd,bkhd->bhqk', xq, xk) * scale
            causal = jnp.tril(jnp.ones((T, T), dtype=bool))
            scores = jnp.where(causal[None, None], scores, NEG_INF)
            probs = jax.nn.softmax(scores.astype(jnp.float32), axis=-1).astype(xq.dtype)
            out = jnp.einsum('bhqk,bkhd->bqhd', probs, xv).reshape(B, T, C)
            return out @ wo.T
        return attention_fwd(x, wq, wk, wv, wo)

    def _L0_cond2_ref(x, c, weight, c_weight, bias):
        import jax, jax.numpy as jnp
        import numpy as np
        from jax import lax
        N, C_IN, L = (32, 64, 1024)
        C_OUT, K, GROUPS = (64, 9, 4)
        C_DIM, PAD, STRIDE = (128, 4, 1)
        out = lax.conv_general_dilated(x, weight, window_strides=(STRIDE,), padding=[(PAD, PAD)], dimension_numbers=('NCH', 'OIH', 'NCH'), feature_group_count=GROUPS)
        ctx = jnp.einsum('nd,od->no', c, c_weight)
        out = out + ctx[:, :, None] + bias[None, :, None]
        return out

    def _L0_ffn_ref(x, A, B, Wr, br):
        import jax, jax.numpy as jnp
        import numpy as np
        ALPHA = 32
        R = 16
        SCALING = ALPHA / R
        H = A.shape[0]
        router_logits = jnp.einsum('bsd,hd->bsh', x, Wr) + br
        scores = H * jax.nn.softmax(router_logits, axis=-1)
        low = jnp.einsum('bsd,hrd->bshr', x, A)
        out = jnp.einsum('bshr,hor,bsh->bso', low, B, scores)
        return SCALING * out
    x = x + _L0_attn_ref(_L0_cond_ref(x, cond_128, L0_cond_W0, L0_cond_b0, L0_cond_W1, L0_cond_b1, L0_cond_W2, L0_cond_b2, L0_cond_weight, L0_cond_bias_k), L0_attn_wq, L0_attn_wk, L0_attn_wv, L0_attn_wo)
    x = x + _L0_ffn_ref(_L0_cond2_ref(x, cond_128, L0_cond2_weight, L0_cond2_c_weight, fside_S_0), L0_ffn_A, L0_ffn_B, L0_ffn_Wr, L0_ffn_br)
    return x

_drawn_inputs = setup_inputs


def setup_inputs(seed=0):
    import zlib

    import numpy as np

    out = dict(_drawn_inputs(seed))
    spreads = {'L0_cond_b0': (0.0, 0.8),
     'L0_cond_b1': (0.0, 0.8),
     'L0_cond_b2': (0.0, 0.8),
     'L0_ffn_br': (0.0, 0.1)}
    factors = {'L0_cond_W0': 2.911, 'L0_cond_bias_k': 5.003, 'L0_attn_wq': 8.0, 'L0_attn_wk': 8.0}
    for name, (base, spread) in spreads.items():
        noise = np.random.default_rng([zlib.crc32(name.encode()), seed]).standard_normal(out[name].shape)
        drawn = base * np.exp(spread * noise) if base else spread * noise
        out[name] = jnp.asarray(drawn.astype(out[name].dtype))
    for name, factor in factors.items():
        out[name] = (out[name] * factor).astype(out[name].dtype)
    return out
```

```python
from contextlib import ExitStack

import concourse.bass as bass
from concourse import mybir

F32 = mybir.dt.float32
ALU = mybir.AluOpType
ACT = mybir.ActivationFunctionType
AX = mybir.AxisListType.X

P = 128
NB = 32
T = 64
D = 1024
NP = NB // 2
NH, HD = 32, 32
C = D // P
BLK = 512
NM = NH // 2
KMIX = 8
HID = 128
TAPS, GROUPS = 9, 4
PH = 4
GC = P // PH
SHIFTS = 3
JB = D // PH // P
XW = D + 2 * PH
EX, R = 8, 16
LOW = EX * R
FFN_SCALE = EX * 32.0 / 16.0
NEG = -1e30


def build(nc, x, condT, W0, b0, W1, b1, W2, b2, mixT, bias_k, wqkvoT, toep, cwT, fside, abT, br, bmT,
          rot, ident, causal, halfsel, pairsel, out):
    SCALE = float(HD) ** -0.5
    ctx = ExitStack()
    with ctx:
        def sb(name, shape):
            return ctx.enter_context(nc.sbuf_tensor(name, shape, F32))

        def sem(name):
            return ctx.enter_context(nc.semaphore(name))

        w = sb("w", [P, C, 4 * D])
        ab = sb("ab", [P, JB, PH, LOW + EX])
        bm = sb("bm", [P, D])
        toe = sb("toe", [P, 2, SHIFTS, P])
        idn = sb("idn", [P, P])
        mask = sb("mask", [P, T])
        cs = sb("cs", [P, 2])
        brb = sb("brb", [P, EX])
        xy = sb("xy", [P, D])
        mixw = sb("mixw", [P, 2 * P])
        cbias = sb("cbias", [P, P])
        yT = sb("yT", [P, C, P])
        rs = sb("rs", [P, 2, BLK])
        qr = sb("qr", [P, D])
        kr = sb("kr", [P, D])
        qoT = sb("qoT", [P, C, P])
        kbd = sb("kbd", [P, 4, 2, 4, T])
        sm = sb("sm", [P, 2, NH // 2, T])
        stat = sb("stat", [P, 2, 3, NH // 2])
        pT = sb("pT", [P, NM, P])
        vbd = sb("vbd", [P, 2, NM, 2, HD])
        x1 = sb("x1", [P, D])
        xrep = sb("xrep", [P, 4, XW])
        cT = sb("cT", [P, JB, PH, P])
        fs = sb("fs", [P, 4 + 3 * EX])
        lows = sb("lows", [P, P])
        lowT = cT[:, 0, 0, :]

        ps = ctx.enter_context(nc.psum_tensor("ps", [P, 8, BLK], F32))
        A = [ps[:, 0, :], ps[:, 1, :]]
        B = ps[:, 2:6, :]
        CC = ps[:, 6:8, :]

        pairc = nc.dram_tensor("pairc", [NP, P, 3 * P], F32, kind="Internal").ap()

        s_small = sem("small_loaded")
        s_const = sem("const_loaded")
        s_w = [sem(f"w{n}_loaded") for n in range(8)]
        s_xy = sem("xy_loaded")
        s_cb = sem("cbias_loaded")
        s_res = sem("residual_loaded")
        s_rep = sem("xrep_loaded")
        s_out = sem("out_stored")
        s_pc = sem("pairc_stored")
        s_ps = sem("setup_pe")
        s_vs = sem("setup_dve")
        s_as = sem("setup_act")
        s_gs = sem("setup_pool")
        names = """y_ready yT_ready qT_ready qT_moved kT_ready k0_act k0_dve k1_act k1_dve
            s0_ready s1_ready conv_ready cT_ready low_ready router_max router_exp router_sum lows_ready
            lowT_ready lowT_moved f_ready result_ready pT0_ready pT1_ready pT0_act pT0_dve pT1_act pT1_dve
            pv_ready oT_ready v0_act v0_dve v1_act v1_dve x1a_ready x1b_ready
            masked0 masked1 max0 max1 shifted0 shifted1 exp0 exp1 sum0 sum1 recip0 recip1 probs0 probs1
            router_sum0 router_w router_e""".split()
        S = {n: sem(n) for n in names}
        s_g = [sem(f"g{n}_ready") for n in range(6)]
        s_sin = [sem(f"sin{n}_ready") for n in range(4)]
        s_rot = [sem(f"rot{n}_ready") for n in range(4)]
        s_wo = [sem(f"wo{n}_ready") for n in range(2)]

        block = ctx.enter_context(nc.Block())

        def steps(eng, step):
            step(0, True, False, False, True)
            step(1, True, True, False, True)
            with eng.Fori(2, NP - 1) as i:
                step(i, True, True, True, True)
            step(NP - 1, True, True, True, False)
            step(NP, False, True, True, False)
            step(NP + 1, False, False, True, False)

        hT = lows[:, 0:NB]
        h2T = lows[:, NB:2 * NB]
        cond = lows[:, 2 * NB:3 * NB]
        w0_s, w1_s = qr[:, 0:HID], qr[:, HID:2 * HID]
        w2_s = qr[:, 2 * HID:2 * HID + KMIX]
        b0_s, b1_s = qr[:, 272:273], qr[:, 273:274]
        b2_s = qr[0:1, 280:280 + KMIX]
        cw_s = qr[:, 288:288 + T]
        bk_s = qr[0:KMIX, 352:352 + T]
        fside_s = qr[0:1, 416:416 + T]
        att = qr[0:NB, 480:480 + KMIX]
        st_s = qr[0:NB, 488:492]
        br_s = qr[0:1, 492:500]
        half_s = kr[0:NB, 0:P]
        psel_s = kr[0:NB, P:P + NP]
        attd = kr[0:NB, 160:160 + NP * KMIX]
        ones = kr[:, 288:288 + P]
        attT = kr[0:KMIX, 416:416 + NB]
        attp = kr[:, 512:512 + NP * KMIX]
        mix_s = x1[:, 0:KMIX * T]
        prod = [sm[:, 0, :, :], sm[:, 1, :, :]]
        accum = pT[:, 0:8, :].rearrange("p a b -> p (a b)").rearrange("p (n t) -> p n t", n=NP)
        spread = cT.rearrange("p a b c -> p (a b c)")
        rows2 = pT.rearrange("p a b -> p (a b)")
        bcast = xrep.rearrange("p a b -> p (a b)")[:, 0:NB * T]
        mixbd = xrep.rearrange("p a b -> p (a b)")[:, NB * T:NB * T + NP * P].rearrange("p (n t) -> p n t", n=NP)

        @block.sync
        def _(sp):
            for dst, src in ((cond, condT), (w0_s, W0), (w1_s, W1), (w2_s, W2), (b0_s, b0), (b1_s, b1), (b2_s, b2),
                             (mix_s[0:T, :], mixT), (mix_s[T:P, :], mixT), (bk_s, bias_k), (cw_s, cwT), (fside_s, fside),
                             (br_s, br), (half_s, halfsel), (psel_s, pairsel), (idn[:, :], ident),
                             (mask[:, :], causal), (cs[:, :], rot)):
                sp.dma_start(dst, src).then_inc(s_small, 16)
            for n in range(8):
                sp.dma_start(w[:, :, n * BLK:(n + 1) * BLK],
                             wqkvoT[n // 2].rearrange("(c p) n -> p c n", p=P)[:, :, n % 2 * BLK:(n % 2 + 1) * BLK]
                             ).then_inc(s_w[n], 16)
                if n == 0:
                    sp.dma_start(xy[:, :], x[0:P, :]).then_inc(s_xy, 16)
            sp.dma_start(ab[:, :, :, :], abT.rearrange("(b j q) n -> j b q n", b=JB, q=PH)).then_inc(s_const, 16)
            sp.dma_start(bm[:, :], bmT).then_inc(s_const, 16)
            sp.dma_start(toe[:, :, :, :], toep).then_inc(s_const, 16)
            dram = pairc.rearrange("n p c -> p n c")
            sp.wait_ge(s_vs, V_MIX)
            sp.dma_start(dram[:, :, 0:P], mixbd).then_inc(s_pc, 16)
            sp.wait_ge(s_as, A_AGGB)
            sp.dma_start(dram[:, :, P:2 * P], bcast.rearrange("p (n c) -> p n c", c=P)).then_inc(s_pc, 16)
            sp.wait_ge(s_pc, 32)
            sp.dma_start(mixw[:, :], pairc[0, :, 0:2 * P]).then_inc(s_xy, 16)
            sp.wait_ge(s_as, A_CTXB)
            sp.dma_start(dram[:, :, 2 * P:3 * P], bcast.rearrange("p (n c) -> p n c", c=P)).then_inc(s_pc, 16)
            sp.wait_ge(s_pc, 48)
            sp.dma_start(cbias[:, :], pairc[0, :, 2 * P:3 * P]).then_inc(s_cb, 16)

            def step(i, proj, attn, tail, more):
                if more:
                    sp.wait_ge(S["y_ready"], i + 1)
                    sp.wait_ge(S["yT_ready"], i + 1)
                    sp.dma_start(xy[:, :], x[bass.ds((i + 1) * P, P), :]).then_inc(s_xy, 16)
                    sp.dma_start(mixw[:, :], pairc[i + 1, :, 0:2 * P]).then_inc(s_xy, 16)
                if tail:
                    if not (isinstance(i, int) and i == NP + 1):
                        sp.wait_ge(S["cT_ready"], i - 1)
                        sp.dma_start(cbias[:, :], pairc[i - 1, :, 2 * P:3 * P]).then_inc(s_cb, 16)
                    sp.wait_ge(S["result_ready"], i - 1)
                    sp.dma_start(out[bass.ds((i - 2) * P, P), :], x1[:, :]).then_inc(s_out, 16)
                if attn:
                    if tail:
                        sp.wait_ge(s_out, 16 * (i - 1))
                    else:
                        sp.wait_ge(s_vs, V_MIX)
                    sp.dma_start(x1[:, :], x[bass.ds((i - 1) * P, P), :]).then_inc(s_res, 16)
                    sp.wait_ge(S["x1b_ready"], i)
                    if tail:
                        sp.wait_ge(S["conv_ready"], i - 1)
                    else:
                        sp.wait_ge(s_pc, 48)
                        sp.wait_ge(s_gs, 4)
                    for q in range(PH):
                        lo, hi = max(0, PH - q), D + PH - q
                        for b in range(4):
                            sp.dma_start(xrep[q * GC:(q + 1) * GC, b, lo:hi],
                                         x1[b * GC:(b + 1) * GC, lo + q - PH:hi + q - PH]).then_inc(s_rep, 16)
            steps(sp, step)
            sp.wait_ge(s_out, 16 * NP)

        REPS = 16 * PH * 4

        @block.gpsimd
        def _(pool):
            pool.memset(ones, 1.0).then_inc(s_gs, 1)
            pool.memset(kbd[:, :, :, :, :], 0.0).then_inc(s_gs, 1)
            pool.memset(vbd[:, :, :, :, :], 0.0).then_inc(s_gs, 1)
            pool.wait_ge(s_pc, 48)
            pool.memset(xrep[:, :, 0:PH], 0.0)
            pool.memset(xrep[:, :, D:XW], 0.0).then_inc(s_gs, 1)

            def half(s, i):
                pool.wait_ge(S[f"masked{s}"], i)
                pool.wait_ge(S[f"max{s}"], i)
                pool.tensor_tensor(sm[:, s, :, :], sm[:, s, :, :],
                                   stat[:, s, 0, :].unsqueeze(2).to_broadcast([P, NH // 2, T]),
                                   ALU.subtract).then_inc(S[f"shifted{s}"], 1)

            def norm(s, i):
                pool.wait_ge(S[f"recip{s}"], i)
                pool.wait_ge(S[f"exp{s}"], i)
                pool.tensor_tensor(sm[:, s, :, :], sm[:, s, :, :],
                                   stat[:, s, 2, :].unsqueeze(2).to_broadcast([P, NH // 2, T]),
                                   ALU.mult).then_inc(S[f"probs{s}"], 1)

            def step(i, proj, attn, tail, more):
                if attn:
                    half(0, i)
                    norm(0, i)
                    half(1, i)
                    norm(1, i)
            steps(pool, step)

        @block.tensor
        def _(pe):
            pe.wait_ge(s_small, 16 * 18)
            pe.matmul(A[0][:, 0:NB], w0_s, cond, start=True, stop=True).then_inc(s_ps, 1)
            pe.wait_ge(s_as, 1)
            pe.matmul(A[1][:, 0:NB], w1_s, hT, start=True, stop=True).then_inc(s_ps, 1)
            pe.wait_ge(s_as, 2)
            pe.wait_ge(s_gs, 1)
            pe.matmul(B[0:NB, 0, 0:KMIX], h2T, w2_s, start=True, stop=False)
            pe.matmul(B[0:NB, 0, 0:KMIX], ones[0:1, 0:NB], b2_s, start=False, stop=True).then_inc(s_ps, 1)
            pe.matmul(B[:, 1, 0:EX], ones[0:1, :], br_s, start=True, stop=True).then_inc(s_ps, 1)
            pe.wait_ge(s_vs, V_ATT)
            pe.transpose(B[0:KMIX, 2, 0:NB], att, idn[0:NB, 0:NB]).then_inc(s_ps, 1)
            pe.wait_ge(s_vs, V_ATTD)
            pe.matmul(B[:, 3, 0:NP * KMIX], half_s, attd, start=True, stop=True).then_inc(s_ps, 1)
            pe.wait_ge(s_vs, V_ROWS)
            for n in range(4):
                pe.matmul(B[:, n, :], ones[0:KMIX, :], rows2[0:KMIX, n * BLK:(n + 1) * BLK], start=True, stop=True
                          ).then_inc(s_ps, 1)
            pe.wait_ge(s_vs, V_CTX)
            pe.wait_ge(s_as, A_AGGB)
            for n in range(4):
                pe.matmul(B[:, n, :], ones, rows2[:, n * BLK:(n + 1) * BLK], start=True, stop=False)
                pe.matmul(B[:, n, :], ones[0:1, :],
                          fside_s.unsqueeze(1).to_broadcast([1, BLK // T, T]), start=False, stop=True).then_inc(s_ps, 1)
            pe.wait_ge(s_as, A_CTXB)

            def mix(p):
                pe.wait_ge(s_xy, 32 * (p + 1))
                for c in range(C):
                    mm = pe.matmul(B[:, c // 4, c % 4 * P:(c % 4 + 1) * P], xy[:, c * P:(c + 1) * P], mixw[:, 0:P],
                                   start=True, stop=True)
                mm.then_inc(S["y_ready"], 1)

            def proj_block(i, n):
                if isinstance(i, int) and i == 0:
                    pe.wait_ge(s_w[n], 16)
                for c in range(C):
                    mm = pe.matmul(A[n % 2], yT[:, c, :], w[:, c, n * BLK:(n + 1) * BLK], start=(c == 0),
                                   stop=(c == C - 1))
                mm.then_inc(s_g[n], 1)

            mix(0)

            def step(i, proj, attn, tail, more):
                if proj:
                    pe.wait_ge(S["yT_ready"], i + 1)
                    if isinstance(i, int) and i == 1:
                        pe.wait_ge(S["v0_act"], 1)
                        pe.wait_ge(S["v0_dve"], 1)
                    elif attn:
                        pe.wait_ge(S["x1a_ready"], i - 1)
                    proj_block(i, 0)
                if attn:
                    pe.wait_ge(s_rot[0], i)
                    pe.wait_ge(s_rot[1], i)
                    for c in range(C):
                        mm = pe.transpose(B[:, c // 4, c % 4 * P:(c % 4 + 1) * P], qr[:, c * P:(c + 1) * P], idn[:, :])
                    mm.then_inc(S["qT_ready"], 1)
                    pe.wait_ge(s_rot[2], i)
                    pe.wait_ge(s_rot[3], i)
                    for c in range(C):
                        mm = pe.transpose(B[:, 2 + c // 4, c % 4 * P:(c % 4 + 1) * P], kr[:, c * P:(c + 1) * P],
                                          idn[:, :])
                    mm.then_inc(S["kT_ready"], 1)
                if proj:
                    if isinstance(i, int) and i == 1:
                        pe.wait_ge(S["v1_act"], 1)
                        pe.wait_ge(S["v1_dve"], 1)
                    elif attn:
                        pe.wait_ge(S["x1b_ready"], i - 1)
                    proj_block(i, 1)

                def scores(s):
                    for c in range(4):
                        for b in range(2):
                            o = B[b * T:(b + 1) * T, 2 * s + c // 2, c % 2 * 256:(c % 2 + 1) * 256]
                            mm = pe.matmul(o, qoT[:, 4 * s + c, b * T:(b + 1) * T],
                                           kbd[:, c, b, :, :].rearrange("p r k -> p (r k)"), start=True, stop=True)
                    mm.then_inc(S[f"s{s}_ready"], 1)

                if attn:
                    pe.wait_ge(S["qT_moved"], i)
                    pe.wait_ge(S["k0_act"], i)
                    pe.wait_ge(S["k0_dve"], i)
                    scores(0)
                if tail:
                    pe.wait_ge(s_rep, REPS * (i - 1))
                    if isinstance(i, int) and i == 2:
                        pe.wait_ge(s_gs, 4)
                        pe.wait_ge(s_const, 48)
                    if attn:
                        pe.wait_ge(S["oT_ready"], i - 1)
                    for jb in range(JB):
                        for b in range(4):
                            o = CC[:, jb, :].rearrange("p (q t) -> p q t", q=PH)[:, :, b * GC:(b + 1) * GC]
                            for d in range(SHIFTS):
                                at = PH * (jb * P + d)
                                mm = pe.matmul(o, xrep[:, b, at:at + PH * (P - 1) + 1:PH],
                                               toe[:, b % 2, d, :].rearrange("p (q t) -> p q t", q=PH),
                                               start=(d == 0), stop=(d == SHIFTS - 1))
                    mm.then_inc(S["conv_ready"], 1)
                if proj:
                    pe.wait_ge(s_rot[0], i + 1)
                    proj_block(i, 2)
                if attn:
                    pe.wait_ge(S["k1_act"], i)
                    pe.wait_ge(S["k1_dve"], i)
                    scores(1)
                if tail:
                    pe.wait_ge(S["cT_ready"], i - 1)
                    for jb in range(JB):
                        for q in range(PH):
                            mm = pe.matmul(CC[:, 0, 0:LOW + EX], cT[:, jb, q, :], ab[:, jb, q, :],
                                           start=(jb + q == 0), stop=(jb == JB - 1 and q == PH - 1))
                    mm.then_inc(S["low_ready"], 1)
                if proj:
                    pe.wait_ge(s_rot[1], i + 1)
                    proj_block(i, 3)
                if tail:
                    pe.wait_ge(S["lows_ready"], i - 1)
                    pe.transpose(CC[:, 1, 0:P], lows[:, :], idn[:, :]).then_inc(S["lowT_ready"], 1)

                def turn_probs(s):
                    pe.wait_ge(S[f"probs{s}"], i)
                    for m in range(8):
                        mm = pe.transpose(B[:, 2 * s + m // 4, m % 4 * P:(m % 4 + 1) * P],
                                          sm[:, s, 2 * m:2 * m + 2, :].rearrange("p h k -> p (h k)"), idn[:, :])
                    mm.then_inc(S[f"pT{s}_ready"], 1)

                if attn:
                    turn_probs(0)
                if proj:
                    pe.wait_ge(s_rot[2], i + 1)
                    proj_block(i, 4)
                if tail:
                    pe.wait_ge(S["lowT_moved"], i - 1)
                    for n in range(2):
                        mm = pe.matmul(CC[:, n, :], lowT, bm[:, n * BLK:(n + 1) * BLK], start=True, stop=True)
                    mm.then_inc(S["f_ready"], 1)
                if attn:
                    turn_probs(1)
                if more:
                    pe.wait_ge(S["pT0_act"], i) if attn else None
                    pe.wait_ge(S["pT0_dve"], i) if attn else None
                    mix(i + 1)
                if attn:
                    pe.wait_ge(S["pT0_act"], i)
                    pe.wait_ge(S["pT0_dve"], i)
                    pe.wait_ge(S["pT1_act"], i)
                    pe.wait_ge(S["pT1_dve"], i)
                    for k in ("v0_act", "v0_dve", "v1_act", "v1_dve"):
                        pe.wait_ge(S[k], i)
                    if tail:
                        pe.wait_ge(S["result_ready"], i - 1)
                    for m in range(NM):
                        for b in range(2):
                            col = m // 2 % 4 * P + b * T
                            mm = pe.matmul(CC[m % 2 * T:(m % 2 + 1) * T, m // 8, col:col + T],
                                           vbd[:, b, m, :, :].rearrange("p a d -> p (a d)"),
                                           pT[:, m, b * T:(b + 1) * T], start=True, stop=True)
                    mm.then_inc(S["pv_ready"], 1)
                if proj:
                    pe.wait_ge(s_rot[3], i + 1)
                    proj_block(i, 5)
                if attn:
                    if isinstance(i, int) and i == 1:
                        pe.wait_ge(s_w[6], 16)
                        pe.wait_ge(s_w[7], 16)
                    pe.wait_ge(S["oT_ready"], i)
                    for n in range(2):
                        if proj:
                            pe.wait_ge(S[f"v{n}_act"], i + 1)
                            pe.wait_ge(S[f"v{n}_dve"], i + 1)
                        for c in range(C):
                            mm = pe.matmul(A[n], qoT[:, c, :], w[:, c, 3 * D + n * BLK:3 * D + (n + 1) * BLK],
                                           start=(c == 0), stop=(c == C - 1))
                        mm.then_inc(s_wo[n], 1)
            steps(pe, step)

        @block.scalar
        def _(act):
            act.wait_ge(s_ps, 1)
            act.activation(hT, A[0][:, 0:NB], ACT.Gelu, bias=b0_s).then_inc(s_as, 1)
            act.wait_ge(s_ps, 2)
            act.activation(h2T, A[1][:, 0:NB], ACT.Gelu, bias=b1_s).then_inc(s_as, 1)
            act.wait_ge(s_vs, 1)
            act.activation(att, B[0:NB, 0, 0:KMIX], ACT.Exp, bias=st_s[:, 0:1], accum_out=st_s[:, 1:2]).then_inc(s_as, 1)
            for n in range(4):
                act.wait_ge(s_ps, 7 + n)
                if n == 0:
                    act.wait_ge(s_vs, V_ROWS)
                act.copy(bcast[:, n * BLK:(n + 1) * BLK], B[:, n, :]).then_inc(s_as, 1)
            act.wait_ge(s_pc, 32)
            for n in range(4):
                act.wait_ge(s_ps, 11 + n)
                act.copy(bcast[:, n * BLK:(n + 1) * BLK], B[:, n, :]).then_inc(s_as, 1)

            act.wait_ge(s_gs, 3)

            def sine(i, n):
                act.wait_ge(s_g[n], i + 1)
                act.wait_ge(s_rot[n % 2 + (2 if n < 2 else 0)], i if n < 2 else i + 1)
                act.activation(rs[:, n % 2, :], A[n % 2], ACT.Copy, scale=cs[:, 1:2]).then_inc(s_sin[n], 1)

            def keys(i, s):
                act.wait_ge(S["kT_ready"], i)
                if s == 1:
                    act.wait_ge(S["s0_ready"], i)
                for r in (0, 2):
                    ins = act.copy(kbd[r * HD:(r + 1) * HD, :, :, r, :],
                                   B[r * HD:(r + 1) * HD, 2 + s, :].rearrange("p (c b k) -> p c b k", c=4, b=2))
                ins.then_inc(S[f"k{s}_act"], 1)

            def values(i, n):
                act.wait_ge(s_g[4 + n], i + 1)
                v = A[n][0:T, :].rearrange("p (m a d) -> p m a d", a=2, d=HD)
                for a in range(2):
                    ins = act.copy(vbd[a * T:(a + 1) * T, 0, 8 * n:8 * n + 8, a, :], v[:, :, a, :])
                ins.then_inc(S[f"v{n}_act"], 1)

            def expo(i, s):
                act.wait_ge(S[f"shifted{s}"], i)
                act.activation(sm[:, s, :, :], sm[:, s, :, :], ACT.Exp, scale=SCALE).then_inc(S[f"exp{s}"], 1)

            def step(i, proj, attn, tail, more):
                if proj:
                    sine(i, 0)
                if attn:
                    act.wait_ge(S["qT_ready"], i)
                    act.copy(qoT[:, :, :], B[:, 0:2, :].rearrange("p a (c t) -> p (a c) t", c=4)
                             ).then_inc(S["qT_moved"], 1)
                    keys(i, 0)
                if proj:
                    sine(i, 1)
                if attn:
                    keys(i, 1)
                    expo(i, 0)
                if proj:
                    sine(i, 2)
                if tail:
                    act.wait_ge(S["router_max"], i - 1)
                    act.activation(fs[:, 4 + EX:4 + 2 * EX], fs[:, 4:4 + EX], ACT.Exp, bias=fs[:, 0:1],
                                   accum_out=fs[:, 1:2]).then_inc(S["router_exp"], 1)
                if attn:
                    expo(i, 1)
                if proj:
                    sine(i, 3)
                if tail:
                    act.wait_ge(S["lowT_ready"], i - 1)
                    act.copy(lowT, CC[:, 1, 0:P]).then_inc(S["lowT_moved"], 1)
                if attn:
                    for s in range(2):
                        act.wait_ge(S[f"pT{s}_ready"], i)
                        act.copy(pT[:, 8 * s:8 * s + 4, :], B[:, 2 * s, :].rearrange("p (m t) -> p m t", m=4)
                                 ).then_inc(S[f"pT{s}_act"], 1)
                    act.wait_ge(S["pv_ready"], i)
                    act.copy(qoT[:, :, :], CC.rearrange("p a (c t) -> p (a c) t", c=4)).then_inc(S["oT_ready"], 1)
                if proj:
                    values(i, 0)
                    values(i, 1)
            steps(act, step)

        @block.vector
        def _(dve):
            n = [0]

            def done(ins):
                n[0] += 1
                ins.then_inc(s_vs, 1)
                dve.wait_ge(s_vs, n[0])
                return n[0]

            dve.wait_ge(s_ps, 3)
            done(dve.tensor_reduce(st_s[:, 0:1], B[0:NB, 0, 0:KMIX], AX, ALU.max, negate=True))
            dve.wait_ge(s_as, 3)
            done(dve.reciprocal(st_s[:, 2:3], st_s[:, 1:2]))
            assert done(dve.tensor_scalar(att, att, st_s[:, 2:3], None, ALU.mult)) == V_ATT
            assert done(dve.tensor_tensor(attd.rearrange("p (n k) -> p n k", k=KMIX),
                                          att.unsqueeze(1).to_broadcast([NB, NP, KMIX]),
                                          psel_s.unsqueeze(2).to_broadcast([NB, NP, KMIX]), ALU.mult)) == V_ATTD
            dve.wait_ge(s_ps, 4)
            done(dve.tensor_copy(brb[:, :], B[:, 1, 0:EX]))
            dve.wait_ge(s_ps, 5)
            done(dve.tensor_copy(attT, B[0:KMIX, 2, 0:NB]))
            dve.wait_ge(s_ps, 6)
            done(dve.tensor_copy(attp, B[:, 3, 0:NP * KMIX]))
            r2 = rows2.rearrange("p (b t) -> p b t", t=T)
            assert done(dve.tensor_tensor(r2[0:KMIX], attT.unsqueeze(2).to_broadcast([KMIX, NB, T]),
                                          bk_s.unsqueeze(1).to_broadcast([KMIX, NB, T]), ALU.mult)) == V_ROWS
            dve.wait_ge(s_ps, 10)
            assert done(dve.tensor_tensor(r2, cond.unsqueeze(2).to_broadcast([P, NB, T]),
                                          cw_s.unsqueeze(1).to_broadcast([P, NB, T]), ALU.mult)) == V_CTX
            ap3 = attp.rearrange("p (n k) -> p n k", k=KMIX)
            acc = cT.rearrange("p a b c -> p (a b c)").rearrange("p (n t) -> p n t", n=NP)
            done(dve.memset(mixbd, 0.0))
            for k in range(KMIX):
                dst = acc if k == 0 else prod[0]
                done(dve.tensor_tensor(dst, mix_s[:, k * T:(k + 1) * T].unsqueeze(1).to_broadcast([P, NP, T]),
                                       ap3[:, :, k].unsqueeze(2).to_broadcast([P, NP, T]), ALU.mult))
                if k:
                    done(dve.tensor_tensor(acc, acc, prod[0], ALU.add))
            done(dve.tensor_copy(mixbd[0:T, :, 0:T], acc[0:T]))
            assert done(dve.tensor_copy(mixbd[T:P, :, T:P], acc[T:P])) == V_MIX

            def mixed(p):
                dve.wait_ge(S["y_ready"], p + 1)
                dve.tensor_tensor(yT[:, :, :], B[:, 0:2, :].rearrange("p a (c t) -> p (a c) t", c=4),
                                  mixw[:, P:2 * P].unsqueeze(1).to_broadcast([P, C, P]), ALU.add
                                  ).then_inc(S["yT_ready"], 1)

            def rotate(i, n):
                dve.wait_ge(s_sin[n], i + 1)
                if attn_of(i):
                    dve.wait_ge(S["qT_ready" if n < 2 else "kT_ready"], i)
                a = A[n % 2].rearrange("p (f e) -> p f e", e=2)
                t = rs[:, n % 2, :].rearrange("p (f e) -> p f e", e=2)
                o = (qr if n < 2 else kr)[:, n % 2 * BLK:(n % 2 + 1) * BLK].rearrange("p (f e) -> p f e", e=2)
                dve.scalar_tensor_tensor(o[:, :, 0], a[:, :, 0], cs[:, 0:1], t[:, :, 1], ALU.mult, ALU.subtract)
                dve.scalar_tensor_tensor(o[:, :, 1], a[:, :, 1], cs[:, 0:1], t[:, :, 0], ALU.mult, ALU.add
                                         ).then_inc(s_rot[n], 1)

            def attn_of(i):
                return not (isinstance(i, int) and i == 0)

            def keys(i, s):
                dve.wait_ge(S["kT_ready"], i)
                if s == 1:
                    dve.wait_ge(S["s0_ready"], i)
                for r in (1, 3):
                    ins = dve.tensor_copy(kbd[r * HD:(r + 1) * HD, :, :, r, :],
                                          B[r * HD:(r + 1) * HD, 2 + s, :].rearrange("p (c b k) -> p c b k", c=4, b=2))
                ins.then_inc(S[f"k{s}_dve"], 1)

            def values(i, n):
                dve.wait_ge(s_g[4 + n], i + 1)
                v = A[n][T:P, :].rearrange("p (m a d) -> p m a d", a=2, d=HD)
                for a in range(2):
                    ins = dve.tensor_copy(vbd[a * T:(a + 1) * T, 1, 8 * n:8 * n + 8, a, :], v[:, :, a, :])
                ins.then_inc(S[f"v{n}_dve"], 1)

            def mask_max(i, s):
                dve.wait_ge(S[f"s{s}_ready"], i)
                dve.tensor_tensor(sm[:, s, :, :], B[:, 2 * s:2 * s + 2, :].rearrange("p a (h k) -> p (a h) k", k=T),
                                  mask[:, :].unsqueeze(1).to_broadcast([P, NH // 2, T]), ALU.add
                                  ).then_inc(S[f"masked{s}"], 1)
                dve.wait_ge(S[f"masked{s}"], i)
                dve.tensor_reduce(stat[:, s, 0, :], sm[:, s, :, :], AX, ALU.max).then_inc(S[f"max{s}"], 1)

            def sums(i, s):
                dve.wait_ge(S[f"exp{s}"], i)
                dve.tensor_reduce(stat[:, s, 1, :], sm[:, s, :, :], AX, ALU.add).then_inc(S[f"sum{s}"], 1)
                dve.wait_ge(S[f"sum{s}"], i)
                dve.reciprocal(stat[:, s, 2, :], stat[:, s, 1, :]).then_inc(S[f"recip{s}"], 1)

            dve.wait_ge(s_xy, 32)
            dve.wait_ge(s_gs, 3)
            mixed(0)

            def step(i, proj, attn, tail, more):
                if proj:
                    rotate(i, 0)
                if attn:
                    keys(i, 0)
                if proj:
                    rotate(i, 1)
                if attn:
                    mask_max(i, 0)
                    keys(i, 1)
                if tail:
                    dve.wait_ge(S["conv_ready"], i - 1)
                    dve.wait_ge(s_cb, 16 * (i - 1))
                    dve.tensor_tensor(cT[:, :, :, :].rearrange("p a q t -> p (a q) t"),
                                      CC.rearrange("p a (q t) -> p (a q) t", q=PH),
                                      cbias[:, :].unsqueeze(1).to_broadcast([P, JB * PH, P]), ALU.add
                                      ).then_inc(S["cT_ready"], 1)
                if attn:
                    sums(i, 0)
                if proj:
                    rotate(i, 2)
                if attn:
                    mask_max(i, 1)
                if tail:
                    dve.wait_ge(S["low_ready"], i - 1)
                    dve.tensor_tensor(fs[:, 4:4 + EX], CC[:, 0, LOW:LOW + EX], brb[:, :], ALU.add
                                      ).then_inc(S["router_sum0"], 1)
                    dve.wait_ge(S["router_sum0"], i - 1)
                    dve.tensor_reduce(fs[:, 0:1], fs[:, 4:4 + EX], AX, ALU.max, negate=True
                                      ).then_inc(S["router_max"], 1)
                if attn:
                    sums(i, 1)
                if tail:
                    dve.wait_ge(S["router_exp"], i - 1)
                    dve.reciprocal(fs[:, 2:3], fs[:, 1:2]).then_inc(S["router_sum"], 1)
                    dve.wait_ge(S["router_sum"], i - 1)
                    dve.tensor_scalar(fs[:, 4 + 2 * EX:4 + 3 * EX], fs[:, 4 + EX:4 + 2 * EX], fs[:, 2:3], FFN_SCALE,
                                      ALU.mult, ALU.mult).then_inc(S["router_w"], 1)
                    dve.wait_ge(S["router_w"], i - 1)
                    dve.tensor_tensor(lows[:, :].rearrange("p (e r) -> p e r", r=R),
                                      CC[:, 0, 0:LOW].rearrange("p (e r) -> p e r", r=R),
                                      fs[:, 4 + 2 * EX:4 + 3 * EX].unsqueeze(2).to_broadcast([P, EX, R]), ALU.mult
                                      ).then_inc(S["lows_ready"], 1)
                if proj:
                    rotate(i, 3)
                if attn:
                    dve.wait_ge(S["pT0_ready"], i)
                    dve.tensor_copy(pT[:, 4:8, :], B[:, 1, :].rearrange("p (m t) -> p m t", m=4)
                                    ).then_inc(S["pT0_dve"], 1)
                if tail:
                    dve.wait_ge(S["f_ready"], i - 1)
                    dve.tensor_tensor(x1[:, :], CC.rearrange("p a c -> p (a c)"), x1[:, :], ALU.add
                                      ).then_inc(S["result_ready"], 1)
                if attn:
                    dve.wait_ge(S["pT1_ready"], i)
                    dve.tensor_copy(pT[:, 12:16, :], B[:, 3, :].rearrange("p (m t) -> p m t", m=4)
                                    ).then_inc(S["pT1_dve"], 1)
                    dve.wait_ge(S["pv_ready"], i)
                if proj:
                    values(i, 0)
                    values(i, 1)
                if more:
                    mixed(i + 1)
                if attn:
                    dve.wait_ge(s_res, 16 * i)
                    for n in range(2):
                        dve.wait_ge(s_wo[n], i)
                        dve.tensor_tensor(x1[:, n * BLK:(n + 1) * BLK], A[n], x1[:, n * BLK:(n + 1) * BLK],
                                          ALU.add).then_inc(S["x1a_ready" if n == 0 else "x1b_ready"], 1)
            steps(dve, step)


V_ATT, V_ATTD, V_ROWS, V_CTX, V_MIX = 3, 4, 8, 9, 27
A_AGGB, A_CTXB = 7, 11

_SHAPES = {}


def kernel(**inputs):
    import numpy as np
    import concourse.bacc as _bacc
    from concourse import mybir as _mybir
    from concourse.bass_utils import run_bass_kernel_spmd as _run

    g = {k: np.asarray(v) for k, v in inputs.items()}

    def c(a):
        return np.ascontiguousarray(a)

    wt = g["L0_cond2_weight"]
    gi = T // GROUPS
    toep = np.zeros((P, 2, SHIFTS, P), wt.dtype)
    for gp in range(2):
        for h in range(2):
            o0 = gp * GC + h * gi
            for ph in range(PH):
                for q in range(PH):
                    for d in range(SHIFTS):
                        k = PH * d + ph - q
                        if 0 <= k < TAPS:
                            toep[ph * GC + h * gi:ph * GC + (h + 1) * gi, gp, d, q * GC + h * gi:q * GC + (h + 1) * gi] = \
                                wt[o0:o0 + gi, :, k].T
    t = np.arange(T, dtype=np.float32)
    arrays = {
        "x": c(g["x"].reshape(NB * T, D)),
        "condT": c(g["cond_128"].T),
        "W0": c(g["L0_cond_W0"]), "b0": c(g["L0_cond_b0"].reshape(HID, 1)),
        "W1": c(g["L0_cond_W1"]), "b1": c(g["L0_cond_b1"].reshape(HID, 1)),
        "W2": c(g["L0_cond_W2"]), "b2": c(g["L0_cond_b2"].reshape(1, KMIX)),
        "mixT": c(g["L0_cond_weight"].reshape(KMIX, T, T).transpose(2, 0, 1).reshape(T, KMIX * T)),
        "bias_k": c(g["L0_cond_bias_k"]),
        "wqkvoT": c(np.stack([g["L0_attn_wq"].T, g["L0_attn_wk"].T, g["L0_attn_wv"].T, g["L0_attn_wo"].T])),
        "toep": toep,
        "cwT": c(g["L0_cond2_c_weight"].T),
        "fside": c(g["fside_S_0"].reshape(1, T)),
        "abT": c(np.concatenate([g["L0_ffn_A"].reshape(LOW, D), g["L0_ffn_Wr"]]).T),
        "br": c(g["L0_ffn_br"].reshape(1, EX)),
        "bmT": c(g["L0_ffn_B"].transpose(0, 2, 1).reshape(LOW, D)),
        "rot": np.tile(np.stack([np.cos(t), np.sin(t)], 1), (2, 1)).astype(np.float32),
        "ident": np.eye(P, dtype=np.float32),
        "causal": np.tile(np.triu(np.full((T, T), NEG, np.float32), 1), (2, 1)),
        "halfsel": (np.arange(NB)[:, None] % 2 == np.arange(P)[None, :] // T).astype(np.float32),
        "pairsel": (np.arange(NB)[:, None] // 2 == np.arange(NP)[None, :]).astype(np.float32),
    }
    nc = _bacc.Bacc("TRN2", target_bir_lowering=False, num_devices=1, dynamic_dma_scratch_size=1024)
    args = {k: nc.dram_tensor(k + "_dram", a.shape, _mybir.dt.from_np(a.dtype), kind="ExternalInput").ap()
            for k, a in arrays.items()}
    out = nc.dram_tensor("out_dram", (NB * T, D), F32, kind="ExternalOutput").ap()
    build(nc, **args, out=out)
    r = _run(nc, [{k + "_dram": a for k, a in arrays.items()}], core_ids=[0])
    return r.results[0]["out_dram"].reshape(NB, T, D)
```

```python
from contextlib import ExitStack

import concourse.bass as bass
from concourse import mybir
import numpy as np

F32 = mybir.dt.float32
F16 = mybir.dt.float16
U32 = mybir.dt.uint32
ALU = mybir.AluOpType
ACT = mybir.ActivationFunctionType
AX = mybir.AxisListType.X

P = 128
NB = 32
T = 64
D = 1024
NP = NB // 2
NH, HD = 32, 32
C = D // P
BLK = 512
NM = NH // 2
KMIX = 8
HID = 128
TAPS, GROUPS = 9, 4
PH = 8
GC = P // PH
NG = P // GC
SHIFTS = 2
PAD = TAPS // 2
PW = D // PH + 1
EX, R = 8, 16
LOW = EX * R
FFN_SCALE = EX * 32.0 / 16.0
NEG = -1e30
NW = 4 * D // BLK
WCOL = C * BLK
EXPO = 0x7F800000
TINY = 2.0 ** -100
TOP = 2.0 ** -13


PACK = {}
for _name, _width in (("W0", HID), ("W1", HID), ("W2", KMIX), ("b0", 1), ("b1", 1), ("cw", T), ("cond", NB),
                      ("mix", KMIX * T), ("halves", P), ("bias_k", T), ("b2", KMIX), ("fside", T),
                      ("br", EX)):
    _at = max((v.stop for v in PACK.values()), default=0)
    PACK[_name] = slice(_at, _at + _width)
PACKED = PACK["br"].stop


def build(nc, x, pack, shapes, mixk, wqkvoT, toep, abT, bmT, out):
    SCALE = float(HD) ** -0.5
    ctx = ExitStack()
    with ctx:
        def sb(name, shape):
            return ctx.enter_context(nc.sbuf_tensor(name, shape, F32))

        def sem(name):
            return ctx.enter_context(nc.semaphore(name))

        arena = sb("arena", [P, NW * WCOL + LATE])
        w = arena[:, 0:NW * WCOL].bitcast(F16).rearrange("p (n h c k) -> p n h c k", n=NW, h=2, c=C)
        xrep, xres, res, toe = (arena[:, NW * WCOL + a:NW * WCOL + b] for a, b in zip(LATE_AT, LATE_AT[1:]))
        xrep = xrep.rearrange("p (b j) -> p b j", b=NG)
        toe = toe.rearrange("p (g d n) -> p g d n", g=GROUPS, d=SHIFTS)

        def raw(n):
            return arena[:, (n + 1) * WCOL:(n + 2) * WCOL].rearrange("p (c k) -> p c k", c=C)

        ab = sb("ab", [P, PH, LOW + EX])
        bm = sb("bm", [P, D])
        kc = sb("kc", [P, P + T + 2])
        idn, mask, cs = kc[:, 0:P], kc[:, P:P + T], kc[:, P + T:P + T + 2]
        brb = sb("brb", [P, EX])
        xy = sb("xy", [P, D])
        mixw = sb("mixw", [P, 2 * P])
        cbias = sb("cbias", [P, P])
        yT = ctx.enter_context(nc.sbuf_tensor("yT", [P, 2, C, P], F16))
        rs = sb("rs", [P, 2, BLK])
        qr = sb("qr", [P, D])
        kr = sb("kr", [P, D])
        qoT = sb("qoT", [P, C, P])
        kbd = sb("kbd", [P, 4, 2, 4, T])
        sm = sb("sm", [P, 2, NH // 2, T])
        stat = sb("stat", [P, 2, 3, NH // 2])
        pT = sb("pT", [P, NM, P])
        vbd = sb("vbd", [P, 2, NM, 2, HD])
        x1 = sb("x1", [P, PH, PW])
        cT = sb("cT", [P, PH, P])
        fs = sb("fs", [P, 4 + 3 * EX])
        lows = sb("lows", [P, P])
        sc = sb("sc", [P, 34])
        rotw, vw, ow = sc[:, 0:8], sc[:, 8:10], sc[:, 10:12]
        y_max, y_all, y_c, y_s, y_h = (sc[:, k:k + 1] for k in range(12, 17))
        rotp, vp = sc[:, 17:25], sc[:, 25:27]
        v_max, v_all, v_c, o_s, o_h = (sc[:, k:k + 1] for k in range(27, 32))
        op = sc[:, 32:34]
        oT = qoT[:, :, :].rearrange("p c t -> p (c t)").bitcast(F16).rearrange("p (h c t) -> p h c t", h=2, c=C)
        y32 = rs[:, :, :].rearrange("p a k -> p (a k)")
        w_max, w_all, w_c, w_s = (lows[:, 96 + 8 * k:104 + 8 * k] for k in range(4))
        lowT = cT[:, 0, :]

        ps = ctx.enter_context(nc.psum_tensor("ps", [P, 8, BLK], F32))
        A = [ps[:, 0, :], ps[:, 1, :]]
        B = ps[:, 2:6, :]
        CC = ps[:, 6:8, :]

        mixd = nc.dram_tensor("mixd", [NP, P, T], F32, kind="Internal").ap()
        x1d = nc.dram_tensor("x1d", [P, PH, PW], F32, kind="Internal").ap()
        biasd = nc.dram_tensor("biasd", [2, NB * T], F32, kind="Internal").ap()

        s_small = sem("small_loaded")
        s_const = sem("const_loaded")
        s_w = [sem(f"w{n}_loaded") for n in range(8)]
        s_mixk = sem("mix_kernels_loaded")
        s_xy = sem("xy_loaded")
        s_cb = sem("cbias_loaded")
        s_res = sem("residual_loaded")
        s_x1 = [sem(f"x1_half{h}_stored") for h in range(2)]
        s_rep = [sem(f"xrep{h}_loaded") for h in range(2)]
        s_out = sem("out_stored")
        s_pb = sem("pair_biases_stored")
        s_pm = sem("pair_mixing_stored")
        s_ps = sem("setup_pe")
        s_vs = sem("setup_dve")
        s_as = sem("setup_act")
        s_gs = sem("setup_pool")
        s_wmax, s_wc, s_ws, s_wh, s_whi, s_wlo0, s_wlo1, s_wconst, s_wsc = (sem("w_" + k) for k in (
            "max_ready", "max_shared", "scale_ready", "inverse_ready", "high_ready", "low_pool_ready",
            "low_dve_ready", "consts_ready", "scaled"))
        s_wall = sem("w_all_ready")
        s_first = sem("first_rotp_ready")
        names = """y_ready yT_ready qT_ready qT_moved kT_ready k0_act k0_dve k1_act k1_dve
            s0_ready s1_ready conv_ready cT_ready low_ready router_max router_exp router_sum lows_ready
            lowT_ready lowT_moved f_ready result_ready pT0_ready pT1_ready pT0_act pT0_dve pT1_act pT1_dve
            pv_ready oT_ready v0_act v0_dve v1_act v1_dve x1a_ready x1b_ready
            masked0 masked1 max0 max1 shifted0 shifted1 exp0 exp1 sum0 sum1 recip0 recip1 probs0 probs1
            router_sum0 router_w
            y32_ready y_max_ready y_all_ready y_c_ready y_s_ready y_h_ready y_high_ready rotp_ready
            v_max_ready v_all_ready v_c_ready o_s_ready o_h_ready op_ready o_high_ready""".split()
        S = {n: sem(n) for n in names}
        s_g = [sem(f"g{n}_ready") for n in range(6)]
        s_sin = [sem(f"sin{n}_ready") for n in range(4)]
        s_rot = [sem(f"rot{n}_ready") for n in range(4)]
        s_wo = [sem(f"wo{n}_ready") for n in range(2)]

        block = ctx.enter_context(nc.Block())

        def steps(eng, step):
            step(0, True, False, False, True)
            step(1, True, True, False, True)
            step(2, True, True, True, True)
            with eng.Fori(3, NP - 1) as i:
                step(i, True, True, True, True)
            step(NP - 1, True, True, True, False)
            step(NP, False, True, True, False)
            step(NP + 1, False, False, True, False)

        hT = lows[:, 0:NB]
        h2T = lows[:, NB:2 * NB]
        small = kbd[:, :, :, :, :].rearrange("p c b r k -> p (c b r k)")

        def packed(name, rows=P):
            return small[0:rows, PACK[name]]

        w0_s, w1_s, w2_s, b0_s, b1_s = (packed(k) for k in ("W0", "W1", "W2", "b0", "b1"))
        cw_s, cond = packed("cw"), packed("cond")
        b2_s, fside_s, br_s = (packed(k, 1) for k in ("b2", "fside", "br"))
        bk_s = packed("bias_k", KMIX)
        mix_s, halves_s = packed("mix"), packed("halves", NB)
        att = small[0:NB, 1200:1200 + KMIX]
        st_s = small[0:NB, 1208:1212]
        attT = small[0:KMIX, 1216:1216 + NB]
        attT0 = small[0:KMIX, 1248:1248 + 2 * P].rearrange("k (h m) -> k h m", h=2)
        att0 = small[:, 1504:1504 + KMIX]
        acc0 = small[:, 1512:1512 + T]
        biases = small[0:NB, 1576:1576 + 2 * T].rearrange("p (a t) -> p a t", a=2)
        ones = small[:, 1704:1704 + P]
        mixk_s = arena[0:KMIX, NW * WCOL:NW * WCOL + T * T]
        mixed_k = [sm[0:NB, :, :, :].rearrange("p a h k -> p (a h k)"), pT[0:NB, :, :].rearrange("p m t -> p (m t)")]

        def bank(n):
            return ps[:, (4, 5, 6, 7, 1, 0, 2, 3)[n], :]

        def load_w(eng, n):
            eng.dma_start(raw(n), wqkvoT[n // 2].rearrange("(c p) n -> p c n", p=P)[:, :, n % 2 * BLK:(n % 2 + 1) * BLK]
                          ).then_inc(s_w[n], 16)

        @block.sync
        def _(sp):
            sp.dma_start(small[:, 0:PACKED], pack).then_inc(s_small, 16)
            sp.dma_start(kc[:, :], shapes).then_inc(s_small, 16)
            sp.dma_start(mixk_s, mixk).then_inc(s_mixk, 16)
            sp.dma_start(xy[:, :], x[0:P, :]).then_inc(s_xy, 16)
            sp.wait_ge(s_small, 32)
            load_w(sp, 0)
            load_w(sp, 1)

            def load_bias(k, p):
                return (mixw[:, P:2 * P] if k == 0 else cbias[:, :]), biasd[k, bass.ds(p * P, P)].partition_broadcast(P)

            sp.wait_ge(s_as, A_CTX)
            sp.wait_ge(s_vs, V_BIAS)
            sp.dma_start(biasd.rearrange("a (b t) -> b a t", t=T), biases).then_inc(s_pb, 16)
            load_w(sp, 2)
            load_w(sp, 3)
            for k in range(2):
                sp.wait_ge(s_as, A_MIX + 4 * k + 4)
                sp.dma_start(mixd.rearrange("n (h i) t -> (n h) (i t)", h=2)[:, k * T * T // 2:(k + 1) * T * T // 2],
                             mixed_k[k]).then_inc(s_pm, 16)
            load_w(sp, 4)

            def step(i, proj, attn, tail, more):
                loads = 16 * i if isinstance(i, int) else sp.snap(sp.to_reg(16 * i))
                if more:
                    first = isinstance(i, int) and i == 0
                    if first:
                        sp.wait_ge(s_pb, 16)
                        sp.wait_ge(s_pm, 32)
                    sp.wait_ge(S["y_ready"], i + 1)
                    sp.wait_ge(S["y32_ready"], i + 1)
                    sp.dma_start(xy[:, :], x[bass.ds((i + 1) * P, P), :]).then_inc(s_xy, 16)
                    for h in range(2):
                        sp.dma_start(mixw[h * T:(h + 1) * T, h * T:(h + 1) * T], mixd[i + 1, h * T:(h + 1) * T, :]
                                     ).then_inc(s_xy, 16)
                    sp.dma_start(*load_bias(0, i + 1)).then_inc(s_xy, 16)
                    if first:
                        sp.dma_start(*load_bias(1, 0)).then_inc(s_cb, 16)
                        for n in range(5, NW):
                            load_w(sp, n)
                        sp.dma_start(ab[:, :, :], abT.rearrange("(j q) n -> j q n", q=PH)).then_inc(s_const, 16)
                        sp.dma_start(bm[:, :], bmT).then_inc(s_const, 16)
                if isinstance(i, int) and i == 1:
                    sp.wait_ge(s_wlo0, NW)
                    sp.wait_ge(s_wlo1, NW)
                    sp.dma_start(toe[:, :, :, :], toep).then_inc(s_const, 16)
                if attn:
                    if tail:
                        sp.wait_ge(S["x1b_ready"], i - 1)
                    sp.dma_start(xres[:, :], x[bass.ds((i - 1) * P, P), :]).then_inc(s_res, 16)
                if tail:
                    if not (isinstance(i, int) and i == NP + 1):
                        sp.wait_ge(S["cT_ready"], i - 1)
                        sp.dma_start(*load_bias(1, i - 1)).then_inc(s_cb, 16)
                    sp.wait_ge(S["result_ready"], i - 1)
                    sp.dma_start(out[bass.ds((i - 2) * P, P), :], res[:, :]).then_inc(s_out, 16)
                if attn:
                    sp.wait_ge(S["x1b_ready"], i)
                    half = slice(0, P // 2), slice(P // 2, P)
                    for h in range(2):
                        sp.dma_start(x1d[half[h]], x1[half[h], :, :]).then_inc(s_x1[h], 16)
                    if tail:
                        sp.wait_ge(S["conv_ready"], i - 1)
                    for h in range(2):
                        sp.wait_ge(s_x1[h], loads)
                        sp.dma_start(xrep[:, h * NG // 2:(h + 1) * NG // 2, :],
                                     x1d[half[h]].rearrange("(b c) q j -> (c q) b j", c=GC)).then_inc(s_rep[h], 16)
            steps(sp, step)
            sp.wait_ge(s_out, 16 * NP)

        @block.gpsimd
        def _(pool):
            pool.memset(ones, 1.0).then_inc(s_gs, 1)
            pool.memset(mixw[:, 0:P], 0.0).then_inc(s_gs, 1)
            pool.memset(vbd[:, :, :, :, :], 0.0).then_inc(s_gs, 1)
            pool.memset(x1[:, 0:PAD, 0], 0.0)
            pool.memset(x1[:, PAD:PH, PW - 1], 0.0).then_inc(s_gs, 1)

            def alone():
                pool.wait_ge(s_gs, 4)

            def share(dst_all, dst_c, src, all_ready, c_ready, k):
                pool.partition_all_reduce(dst_all, src, P, bass.bass_isa.ReduceOp.max).then_inc(all_ready, 1)
                alone()
                pool.wait_ge(all_ready, k)
                pool.tensor_scalar(dst_c, dst_all, TINY, TOP, ALU.max, ALU.mult).then_inc(c_ready, 1)

            def share_w(n):
                alone()
                pool.wait_ge(s_wmax, n + 1)
                share(w_all[:, n:n + 1], w_c[:, n:n + 1], w_max[:, n:n + 1], s_wall, s_wc, n + 1)

            def w_consts(n):
                pool.wait_ge(s_wh, n + 1)
                h = w_c[:, n:n + 1]
                if n < 4:
                    pool.tensor_scalar(rotw[:, 2 * n:2 * n + 2], cs[:, :], h, 0.25, ALU.mult, ALU.mult).then_inc(s_wconst, 1)
                else:
                    dst = vw if n < 6 else ow
                    pool.tensor_scalar(dst[:, n % 2:n % 2 + 1], h, 0.25, None, ALU.mult).then_inc(s_wconst, 1)


            def share_y(own):
                alone()
                pool.wait_ge(S["y_max_ready"], own)
                share(y_all, y_c, y_max, S["y_all_ready"], S["y_c_ready"], own)

            def pair_consts(own, last):
                alone()
                pool.wait_ge(S["y_h_ready"], own)
                pool.wait_ge(S["v1_act"], last)
                pool.wait_ge(S["v1_dve"], last)
                pool.tensor_scalar(sc[:, 17:27], sc[:, 0:10], y_h, None, ALU.mult).then_inc(S["rotp_ready"], 1)

            def share_v(own):
                alone()
                pool.wait_ge(S["v_max_ready"], own)
                share(v_all, v_c, v_max, S["v_all_ready"], S["v_c_ready"], own)

            def out_consts(own, last):
                alone()
                pool.wait_ge(S["o_h_ready"], own)
                if last is not None:
                    pool.wait_ge(S["x1b_ready"], last)
                pool.tensor_scalar(op, ow, o_h, None, ALU.mult).then_inc(S["op_ready"], 1)

            def half(s, i):
                pool.wait_ge(S[f"masked{s}"], i)
                pool.wait_ge(S[f"max{s}"], i)
                pool.tensor_tensor(sm[:, s, :, :], sm[:, s, :, :],
                                   stat[:, s, 0, :].unsqueeze(2).to_broadcast([P, NH // 2, T]),
                                   ALU.subtract).then_inc(S[f"shifted{s}"], 1)

            def norm(s, i):
                pool.wait_ge(S[f"recip{s}"], i)
                pool.wait_ge(S[f"exp{s}"], i)
                pool.tensor_tensor(sm[:, s, :, :], sm[:, s, :, :],
                                   stat[:, s, 2, :].unsqueeze(2).to_broadcast([P, NH // 2, T]),
                                   ALU.mult).then_inc(S[f"probs{s}"], 1)

            def low_w(n):
                pool.wait_ge(s_whi, 2 * n + 1)
                if n:
                    pool.wait_ge(s_wlo1, n)
                cc = slice(0, C // 2)
                pool.tensor_tensor(w[:, n, 1, cc, :], raw(n)[:, cc, :], w[:, n, 0, cc, :], ALU.subtract
                                   ).then_inc(s_wlo0, 1)

            def first_consts(n):
                pool.wait_ge(S["y_h_ready"], 1)
                pool.wait_ge(s_wconst, n + 1)
                k = slice(2 * n, 2 * n + 2) if n < 4 else slice(4 + n, 5 + n)
                pool.tensor_scalar(sc[:, 17:27][:, k], sc[:, 0:10][:, k], y_h, None, ALU.mult).then_inc(s_first, 1)

            share_w(0)
            w_consts(0)
            share_y(1)
            low_w(0)
            first_consts(0)
            for n in range(1, 6):
                share_w(n)
                w_consts(n)
                first_consts(n)
                low_w(n)

            def step(i, proj, attn, tail, more):
                if isinstance(i, int) and i == 0:
                    share_w(6)
                    w_consts(6)
                last, own, ahead = (c if isinstance(i, int) else pool.snap(pool.to_reg(c)) for c in (i - 1, i + 1, i + 2))
                if attn:
                    if isinstance(i, int) and i == 1:
                        w_consts(7)
                        pool.wait_ge(s_wconst, NW)
                    out_consts(i, last if tail else None)
                    half(0, i)
                    norm(0, i)
                    half(1, i)
                    norm(1, i)
                if isinstance(i, int) and i == 1:
                    low_w(7)
                if more:
                    share_y(ahead)
                    pair_consts(ahead, own)
                if isinstance(i, int) and i == 0:
                    pool.wait_ge(s_ps, PE_MIX)
                    pool.wait_ge(s_pb, 16)
                    pool.memset(kbd[:, :, :, :, :], 0.0).then_inc(s_gs, 1)
                if isinstance(i, int) and i == 0:
                    low_w(6)
                    share_w(7)
                if proj:
                    share_v(own)
            steps(pool, step)

        @block.tensor
        def _(pe):
            pe.wait_ge(s_small, 32)
            pe.matmul(A[0][:, 0:NB], w0_s, cond, start=True, stop=True).then_inc(s_ps, 1)
            pe.wait_ge(s_gs, 1)
            pe.matmul(B[0:NB, 1, 0:T], cond, cw_s, start=True, stop=False)
            pe.matmul(B[0:NB, 1, 0:T], ones[0:1, 0:NB], fside_s, start=False, stop=True).then_inc(s_ps, 1)
            pe.matmul(B[:, 2, 0:EX], ones[0:1, :], br_s, start=True, stop=True).then_inc(s_ps, 1)
            pe.wait_ge(s_as, 1)
            pe.matmul(A[1][:, 0:NB], w1_s, hT, start=True, stop=True).then_inc(s_ps, 1)
            pe.wait_ge(s_as, 3)
            pe.matmul(B[0:NB, 0, 0:KMIX], h2T, w2_s, start=True, stop=False)
            pe.matmul(B[0:NB, 0, 0:KMIX], ones[0:1, 0:NB], b2_s, start=False, stop=True).then_inc(s_ps, 1)
            pe.wait_ge(s_vs, V_ATT)
            pe.transpose(B[0:KMIX, 3, 0:NB], att, idn[0:NB, 0:NB]).then_inc(s_ps, 1)
            pe.matmul(A[1][:, 0:KMIX], halves_s, att, start=True, stop=True).then_inc(s_ps, 1)
            pe.wait_ge(s_vs, V_ATTT)
            pe.matmul(A[0][0:NB, 0:T], attT, bk_s, start=True, stop=True)
            for h in range(2):
                mm = pe.matmul(A[0][:, (h + 1) * T:(h + 2) * T], attT0[:, h, :], bk_s, start=True, stop=True)
            mm.then_inc(s_ps, 1)

            def mix(p):
                pe.wait_ge(s_xy, 64 * p + 16)
                for c in range(C):
                    mm = pe.matmul(B[:, c // 4, c % 4 * P:(c % 4 + 1) * P], xy[:, c * P:(c + 1) * P], mixw[:, 0:P],
                                   start=True, stop=True)
                mm.then_inc(S["y_ready"], 1)

            def proj_block(i, n):
                if isinstance(i, int) and i == 0:
                    pe.wait_ge(s_as, A_MIX + 8)
                    pe.wait_ge(s_wlo0, n + 1)
                    pe.wait_ge(s_wlo1, n + 1)
                split_matmul(A[n % 2], yT, n).then_inc(s_g[n], 1)

            def split_matmul(o, v, n):
                for c in range(C):
                    pe.matmul(o, v[:, 0, c, :], w[:, n, 0, c, :], start=(c == 0), stop=False)
                    pe.matmul(o, v[:, 0, c, :], w[:, n, 1, c, :], start=False, stop=False)
                    mm = pe.matmul(o, v[:, 1, c, :], w[:, n, 0, c, :], start=False, stop=(c == C - 1))
                return mm

            def mixed_kernels(n):
                pe.matmul(bank(n)[0:NB, :], attT, mixk_s[:, n * BLK:(n + 1) * BLK], start=True, stop=True
                          ).then_inc(s_ps, 1)

            pe.wait_ge(s_mixk, 16)
            for n in range(2):
                mixed_kernels(n)
            pe.wait_ge(s_vs, V_MIX0)
            mix(0)
            for n in range(2, 8):
                if n == 4:
                    pe.wait_ge(s_vs, V_BIAS + 1)
                if n == 6:
                    pe.wait_ge(S["y32_ready"], 1)
                mixed_kernels(n)
            def step(i, proj, attn, tail, more):
                if proj:
                    pe.wait_ge(S["yT_ready"], i + 1)
                    if isinstance(i, int) and i == 1:
                        pe.wait_ge(S["v0_act"], 1)
                        pe.wait_ge(S["v0_dve"], 1)
                    elif attn:
                        pe.wait_ge(S["x1a_ready"], i - 1)
                    proj_block(i, 0)
                if attn:
                    pe.wait_ge(s_rot[0], i)
                    pe.wait_ge(s_rot[1], i)
                    for c in range(C):
                        mm = pe.transpose(B[:, c // 4, c % 4 * P:(c % 4 + 1) * P], qr[:, c * P:(c + 1) * P], idn[:, :])
                    mm.then_inc(S["qT_ready"], 1)
                    pe.wait_ge(s_rot[2], i)
                    pe.wait_ge(s_rot[3], i)
                    for c in range(C):
                        mm = pe.transpose(B[:, 2 + c // 4, c % 4 * P:(c % 4 + 1) * P], kr[:, c * P:(c + 1) * P],
                                          idn[:, :])
                    mm.then_inc(S["kT_ready"], 1)
                if proj:
                    if isinstance(i, int) and i == 1:
                        pe.wait_ge(S["v1_act"], 1)
                        pe.wait_ge(S["v1_dve"], 1)
                    elif attn:
                        pe.wait_ge(S["x1b_ready"], i - 1)
                    proj_block(i, 1)

                def scores(s):
                    for c in range(4):
                        for b in range(2):
                            o = B[b * T:(b + 1) * T, 2 * s + c // 2, c % 2 * 256:(c % 2 + 1) * 256]
                            mm = pe.matmul(o, qoT[:, 4 * s + c, b * T:(b + 1) * T],
                                           kbd[:, c, b, :, :].rearrange("p r k -> p (r k)"), start=True, stop=True)
                    mm.then_inc(S[f"s{s}_ready"], 1)

                if attn:
                    pe.wait_ge(S["qT_moved"], i)
                    pe.wait_ge(S["k0_act"], i)
                    pe.wait_ge(S["k0_dve"], i)
                    scores(0)
                    if not proj:
                        pe.wait_ge(S["k1_act"], i)
                        pe.wait_ge(S["k1_dve"], i)
                        scores(1)
                if tail:
                    if isinstance(i, int) and i == 2:
                        pe.wait_ge(s_const, 48)
                    if attn:
                        pe.wait_ge(S["oT_ready"], i - 1)
                    for b in range(NG):
                        if b % (NG // 2) == 0:
                            pe.wait_ge(s_rep[b // (NG // 2)], 16 * (i - 1))
                        o = CC.rearrange("p a (b n) -> p (a b) n", n=P)[:, b, :]
                        for d in range(SHIFTS):
                            mm = pe.matmul(o, xrep[:, b, d:d + P], toe[:, b % GROUPS, d, :],
                                           start=(d == 0), stop=(d == SHIFTS - 1))
                    mm.then_inc(S["conv_ready"], 1)
                if proj:
                    pe.wait_ge(s_rot[0], i + 1)
                    proj_block(i, 2)
                if attn and proj:
                    pe.wait_ge(S["k1_act"], i)
                    pe.wait_ge(S["k1_dve"], i)
                    scores(1)
                if tail:
                    pe.wait_ge(S["cT_ready"], i - 1)
                    for q in range(PH):
                        mm = pe.matmul(CC[:, 0, 0:LOW + EX], cT[:, q, :], ab[:, q, :], start=(q == 0), stop=(q == PH - 1))
                    mm.then_inc(S["low_ready"], 1)
                if isinstance(i, int) and i == 0:
                    mix(1)
                if proj:
                    pe.wait_ge(s_rot[1], i + 1)
                    proj_block(i, 3)

                def turn_probs(s):
                    pe.wait_ge(S[f"probs{s}"], i)
                    for m in range(8):
                        mm = pe.transpose(B[:, 2 * s + m // 4, m % 4 * P:(m % 4 + 1) * P],
                                          sm[:, s, 2 * m:2 * m + 2, :].rearrange("p h k -> p (h k)"), idn[:, :])
                    mm.then_inc(S[f"pT{s}_ready"], 1)

                if attn:
                    turn_probs(0)
                if tail:
                    pe.wait_ge(S["lows_ready"], i - 1)
                    pe.transpose(CC[:, 1, 0:P], lows[:, :], idn[:, :]).then_inc(S["lowT_ready"], 1)
                if proj:
                    pe.wait_ge(s_rot[2], i + 1)
                    proj_block(i, 4)
                if tail:
                    pe.wait_ge(S["lowT_moved"], i - 1)
                    for n in range(2):
                        mm = pe.matmul(CC[:, n, :], lowT, bm[:, n * BLK:(n + 1) * BLK], start=True, stop=True)
                    mm.then_inc(S["f_ready"], 1)
                if attn:
                    turn_probs(1)
                if more and attn:
                    pe.wait_ge(S["pT0_act"], i)
                    pe.wait_ge(S["pT0_dve"], i)
                    mix(i + 1)
                if attn:
                    pe.wait_ge(S["pT0_act"], i)
                    pe.wait_ge(S["pT0_dve"], i)
                    pe.wait_ge(S["pT1_act"], i)
                    pe.wait_ge(S["pT1_dve"], i)
                    for k in ("v0_act", "v0_dve", "v1_act", "v1_dve"):
                        pe.wait_ge(S[k], i)
                    if tail:
                        pe.wait_ge(S["result_ready"], i - 1)
                    for m in range(NM):
                        for b in range(2):
                            col = m // 2 % 4 * P + b * T
                            mm = pe.matmul(CC[m % 2 * T:(m % 2 + 1) * T, m // 8, col:col + T],
                                           vbd[:, b, m, :, :].rearrange("p a d -> p (a d)"),
                                           pT[:, m, b * T:(b + 1) * T], start=True, stop=True)
                    mm.then_inc(S["pv_ready"], 1)
                if proj:
                    pe.wait_ge(s_rot[3], i + 1)
                    proj_block(i, 5)
                if attn:
                    if isinstance(i, int) and i == 1:
                        pe.wait_ge(s_wlo0, NW)
                        pe.wait_ge(s_wlo1, NW)
                    pe.wait_ge(S["oT_ready"], i)
                    for n in range(2):
                        if proj:
                            pe.wait_ge(S[f"v{n}_act"], i + 1)
                            pe.wait_ge(S[f"v{n}_dve"], i + 1)
                        split_matmul(A[n], oT, 6 + n).then_inc(s_wo[n], 1)
            steps(pe, step)

        @block.scalar
        def _(act):
            act.wait_ge(s_small, 32)
            act.wait_ge(s_ps, 1)
            act.activation(hT, A[0][:, 0:NB], ACT.Gelu, bias=b0_s).then_inc(s_as, 1)
            act.wait_ge(s_ps, 2)
            act.copy(biases[:, 1, :], B[0:NB, 1, 0:T]).then_inc(s_as, 1)
            act.wait_ge(s_ps, 4)
            act.activation(h2T, A[1][:, 0:NB], ACT.Gelu, bias=b1_s).then_inc(s_as, 1)
            act.wait_ge(s_vs, 2)
            act.activation(att, B[0:NB, 0, 0:KMIX], ACT.Exp, bias=st_s[:, 0:1], accum_out=st_s[:, 1:2]).then_inc(s_as, 1)

            def mixed_kernels(n):
                act.wait_ge(s_ps, PE_MIX + n + 1)
                act.copy(mixed_k[n // 4][:, n % 4 * BLK:(n % 4 + 1) * BLK], bank(n)[0:NB, :]).then_inc(s_as, 1)

            def high_w(n, *halves):
                for h in halves or range(2):
                    cc = slice(h * C // 2, (h + 1) * C // 2)
                    scale = w_s[:, n:n + 1]
                    if h == 0:
                        act.wait_ge(s_ws, n + 1)
                        act.activation(raw(n)[:, cc, :], raw(n)[:, cc, :], ACT.Copy, scale=scale).then_inc(s_wsc, 1)
                        act.wait_ge(s_wsc, n + 1)
                        scale = 1.0
                        if n:
                            act.wait_ge(s_wlo0, n)
                    act.activation(w[:, n, 0, cc, :], raw(n)[:, cc, :], ACT.Copy, scale=scale).then_inc(s_whi, 1)

            def high_y(p):
                act.wait_ge(S["y_s_ready"], p + 1)
                if not (isinstance(p, int) and p == 0):
                    act.wait_ge(s_g[5], p)
                act.activation(yT[:, 0, :, :].rearrange("p c t -> p (c t)"), y32, ACT.Copy, scale=y_s
                               ).then_inc(S["y_high_ready"], 1)

            for n in range(2):
                mixed_kernels(n)
            high_w(0, 0)
            high_y(0)
            high_w(0, 1)
            for n in range(2, 8):
                mixed_kernels(n)
            high_w(1)

            act.wait_ge(s_gs, 3)

            def sine(i, n):
                act.wait_ge(s_g[n], i + 1)
                if isinstance(i, int) and i == 0:
                    act.wait_ge(s_first, n + 1)
                else:
                    act.wait_ge(S["rotp_ready"], i)
                if n < 2:
                    act.wait_ge(S["yT_ready"], i + 1)
                else:
                    act.wait_ge(s_rot[n - 2], i + 1)
                act.activation(rs[:, n % 2, :], A[n % 2], ACT.Copy, scale=rotp[:, 2 * n + 1:2 * n + 2]
                               ).then_inc(s_sin[n], 1)

            def keys(i, s):
                act.wait_ge(S["kT_ready"], i)
                if isinstance(i, int) and i == 1:
                    act.wait_ge(s_gs, 5)
                if s == 1:
                    act.wait_ge(S["s0_ready"], i)
                for r in (0, 2):
                    ins = act.copy(kbd[r * HD:(r + 1) * HD, :, :, r, :],
                                   B[r * HD:(r + 1) * HD, 2 + s, :].rearrange("p (c b k) -> p c b k", c=4, b=2))
                ins.then_inc(S[f"k{s}_act"], 1)

            def values(i, n):
                act.wait_ge(s_g[4 + n], i + 1)
                if isinstance(i, int) and i == 0:
                    act.wait_ge(s_first, 5 + n)
                v = A[n][0:T, :].rearrange("p (m a d) -> p m a d", a=2, d=HD)
                for a in range(2):
                    ins = act.activation(vbd[a * T:(a + 1) * T, 0, 8 * n:8 * n + 8, a, :], v[:, :, a, :], ACT.Copy,
                                         scale=vp[0:T, n:n + 1])
                ins.then_inc(S[f"v{n}_act"], 1)

            def expo(i, s):
                act.wait_ge(S[f"shifted{s}"], i)
                act.activation(sm[:, s, :, :], sm[:, s, :, :], ACT.Exp, scale=SCALE).then_inc(S[f"exp{s}"], 1)

            def step(i, proj, attn, tail, more):
                first = isinstance(i, int) and i == 0
                if proj:
                    sine(i, 0)
                if first:
                    high_w(2)
                if attn:
                    act.wait_ge(S["qT_ready"], i)
                    act.copy(qoT[:, :, :], B[:, 0:2, :].rearrange("p a (c t) -> p (a c) t", c=4)
                             ).then_inc(S["qT_moved"], 1)
                    keys(i, 0)
                if proj:
                    sine(i, 1)
                if first:
                    high_w(3)
                if attn:
                    keys(i, 1)
                    expo(i, 0)
                if proj:
                    sine(i, 2)
                if isinstance(i, int) and i == 1:
                    high_w(7)
                if first:
                    high_w(4)
                if tail:
                    act.wait_ge(S["router_max"], i - 1)
                    act.activation(fs[:, 4 + EX:4 + 2 * EX], fs[:, 4:4 + EX], ACT.Exp, bias=fs[:, 0:1],
                                   accum_out=fs[:, 1:2]).then_inc(S["router_exp"], 1)
                if attn:
                    expo(i, 1)
                if proj:
                    sine(i, 3)
                if first:
                    high_w(5)
                if tail:
                    act.wait_ge(S["lowT_ready"], i - 1)
                    act.copy(lowT, CC[:, 1, 0:P]).then_inc(S["lowT_moved"], 1)
                if attn:
                    for s in range(2):
                        act.wait_ge(S[f"pT{s}_ready"], i)
                        act.copy(pT[:, 8 * s:8 * s + 4, :], B[:, 2 * s, :].rearrange("p (m t) -> p m t", m=4)
                                 ).then_inc(S[f"pT{s}_act"], 1)
                    act.wait_ge(S["pv_ready"], i)
                    act.wait_ge(S["o_s_ready"], i)
                    act.activation(oT[:, 0, :, :], CC.rearrange("p a (c t) -> p (a c) t", c=4), ACT.Copy, scale=o_s
                                   ).then_inc(S["o_high_ready"], 1)
                if proj:
                    values(i, 0)
                    values(i, 1)
                if more:
                    high_y(i + 1)
                if first:
                    high_w(6)
            steps(act, step)

        @block.vector
        def _(dve):
            n = [0]

            def done(ins):
                n[0] += 1
                ins.then_inc(s_vs, 1)
                dve.wait_ge(s_vs, n[0])
                return n[0]

            def scales(s_out, h_out, c, s_ready, h_ready):
                dve.tensor_scalar(s_out.bitcast(U32), c.bitcast(U32), EXPO, EXPO, ALU.bitwise_and, ALU.bitwise_xor
                                  ).then_inc(s_ready, 1)
                return dve.tensor_scalar(h_out.bitcast(U32), c.bitcast(U32), EXPO, None, ALU.bitwise_and
                                         ).then_inc(h_ready, 1)

            def max_w(n):
                dve.wait_ge(s_w[n], 16)
                dve.tensor_reduce(w_max[:, n:n + 1], raw(n), mybir.AxisListType.XY, ALU.max, apply_absolute_value=True
                                  ).then_inc(s_wmax, 1)

            def scale_w(n):
                dve.wait_ge(s_wc, n + 1)
                scales(w_s[:, n:n + 1], w_c[:, n:n + 1], w_c[:, n:n + 1], s_ws, s_wh)

            def low_w(n):
                dve.wait_ge(s_whi, 2 * n + 2)
                if n:
                    dve.wait_ge(s_wlo1, n)
                cc = slice(C // 2, C)
                dve.scalar_tensor_tensor(w[:, n, 1, cc, :], raw(n)[:, cc, :], w_s[:, n:n + 1], w[:, n, 0, cc, :],
                                         ALU.mult, ALU.subtract).then_inc(s_wlo1, 1)

            dve.wait_ge(s_ps, 3)
            done(dve.tensor_copy(brb[:, :], B[:, 2, 0:EX]))
            dve.wait_ge(s_ps, 5)
            done(dve.tensor_reduce(st_s[:, 0:1], B[0:NB, 0, 0:KMIX], AX, ALU.max, negate=True))
            dve.wait_ge(s_as, 4)
            done(dve.reciprocal(st_s[:, 2:3], st_s[:, 1:2]))
            assert done(dve.tensor_scalar(att, att, st_s[:, 2:3], None, ALU.mult)) == V_ATT
            dve.wait_ge(s_ps, 6)
            assert done(dve.tensor_copy(attT, B[0:KMIX, 3, 0:NB])) == V_ATTT - 1
            assert done(dve.tensor_copy(attT0, attT[:, 0:2].unsqueeze(2).to_broadcast([KMIX, 2, P]))) == V_ATTT
            dve.wait_ge(s_ps, 7)
            done(dve.tensor_copy(att0, A[1][:, 0:KMIX]))
            done(dve.tensor_scalar(acc0, mix_s[:, 0:T], att0[:, 0:1], None, ALU.mult))
            for k in range(1, KMIX):
                done(dve.scalar_tensor_tensor(acc0, mix_s[:, k * T:(k + 1) * T], att0[:, k:k + 1], acc0, ALU.mult,
                                              ALU.add))
            dve.wait_ge(s_gs, 2)
            done(dve.tensor_copy(mixw[0:T, 0:T], acc0[0:T]))
            assert done(dve.tensor_copy(mixw[T:P, T:P], acc0[T:P])) == V_MIX0
            dve.wait_ge(s_ps, 8)
            assert done(dve.tensor_copy(biases[:, 0, :], A[0][0:NB, 0:T])) == V_BIAS
            done(dve.tensor_copy(mixw[:, P:2 * P], A[0][:, T:3 * T]))

            def mixed(p):
                dve.wait_ge(S["y_ready"], p + 1)
                if isinstance(p, int) and p == 1:
                    dve.wait_ge(s_rot[3], p)
                dve.tensor_tensor(y32.rearrange("p (c t) -> p c t", c=C), B[:, 0:2, :].rearrange("p a (c t) -> p (a c) t", c=4),
                                  mixw[:, P:2 * P].unsqueeze(1).to_broadcast([P, C, P]), ALU.add
                                  ).then_inc(S["y32_ready"], 1)
                dve.wait_ge(S["y32_ready"], p + 1)
                dve.tensor_reduce(y_max, y32, AX, ALU.max, apply_absolute_value=True).then_inc(S["y_max_ready"], 1)

            def scale_y(p):
                dve.wait_ge(S["y_c_ready"], p + 1)
                if not (isinstance(p, int) and p <= 1):
                    dve.wait_ge(S["rotp_ready"], p - 1)
                elif p == 1:
                    dve.wait_ge(s_first, 6)
                scales(y_s, y_h, y_c, S["y_s_ready"], S["y_h_ready"])

            def low_y(p):
                dve.wait_ge(S["y_high_ready"], p + 1)
                dve.scalar_tensor_tensor(yT[:, 1, :, :].rearrange("p c t -> p (c t)"), y32, y_s,
                                         yT[:, 0, :, :].rearrange("p c t -> p (c t)"), ALU.mult, ALU.subtract
                                         ).then_inc(S["yT_ready"], 1)

            def scale_o(p):
                for k in ("v0_act", "v0_dve", "v1_act", "v1_dve"):
                    dve.wait_ge(S[k], p + 1)
                dve.tensor_reduce(v_max, vbd[:, :, :, :, :].rearrange("p b m a d -> p (b m a d)"), AX, ALU.max,
                                  apply_absolute_value=True).then_inc(S["v_max_ready"], 1)
                dve.wait_ge(S["v_c_ready"], p + 1)
                if not (isinstance(p, int) and p == 0):
                    dve.wait_ge(S["op_ready"], p)
                scales(o_s, o_h, v_c, S["o_s_ready"], S["o_h_ready"])

            def rotate(i, n):
                dve.wait_ge(s_sin[n], i + 1)
                if attn_of(i):
                    dve.wait_ge(S["qT_ready" if n < 2 else "kT_ready"], i)
                a = A[n % 2].rearrange("p (f e) -> p f e", e=2)
                t = rs[:, n % 2, :].rearrange("p (f e) -> p f e", e=2)
                o = (qr if n < 2 else kr)[:, n % 2 * BLK:(n % 2 + 1) * BLK].rearrange("p (f e) -> p f e", e=2)
                cos = rotp[:, 2 * n:2 * n + 1]
                dve.scalar_tensor_tensor(o[:, :, 0], a[:, :, 0], cos, t[:, :, 1], ALU.mult, ALU.subtract)
                dve.scalar_tensor_tensor(o[:, :, 1], a[:, :, 1], cos, t[:, :, 0], ALU.mult, ALU.add
                                         ).then_inc(s_rot[n], 1)

            def attn_of(i):
                return not (isinstance(i, int) and i == 0)

            def keys(i, s):
                dve.wait_ge(S["kT_ready"], i)
                if isinstance(i, int) and i == 1:
                    dve.wait_ge(s_gs, 5)
                if s == 1:
                    dve.wait_ge(S["s0_ready"], i)
                for r in (1, 3):
                    ins = dve.tensor_copy(kbd[r * HD:(r + 1) * HD, :, :, r, :],
                                          B[r * HD:(r + 1) * HD, 2 + s, :].rearrange("p (c b k) -> p c b k", c=4, b=2))
                ins.then_inc(S[f"k{s}_dve"], 1)

            def values(i, n):
                dve.wait_ge(s_g[4 + n], i + 1)
                if isinstance(i, int) and i == 0:
                    dve.wait_ge(s_first, 5 + n)
                v = A[n][T:P, :].rearrange("p (m a d) -> p m a d", a=2, d=HD)
                for a in range(2):
                    ins = dve.tensor_scalar(vbd[a * T:(a + 1) * T, 1, 8 * n:8 * n + 8, a, :], v[:, :, a, :],
                                            vp[T:P, n:n + 1], None, ALU.mult)
                ins.then_inc(S[f"v{n}_dve"], 1)

            def mask_max(i, s):
                dve.wait_ge(S[f"s{s}_ready"], i)
                dve.tensor_tensor(sm[:, s, :, :], B[:, 2 * s:2 * s + 2, :].rearrange("p a (h k) -> p (a h) k", k=T),
                                  mask[:, :].unsqueeze(1).to_broadcast([P, NH // 2, T]), ALU.add
                                  ).then_inc(S[f"masked{s}"], 1)
                dve.wait_ge(S[f"masked{s}"], i)
                dve.tensor_reduce(stat[:, s, 0, :], sm[:, s, :, :], AX, ALU.max).then_inc(S[f"max{s}"], 1)

            def sums(i, s):
                dve.wait_ge(S[f"exp{s}"], i)
                dve.tensor_reduce(stat[:, s, 1, :], sm[:, s, :, :], AX, ALU.add).then_inc(S[f"sum{s}"], 1)
                dve.wait_ge(S[f"sum{s}"], i)
                dve.reciprocal(stat[:, s, 2, :], stat[:, s, 1, :]).then_inc(S[f"recip{s}"], 1)

            max_w(0)
            scale_w(0)
            mixed(0)
            scale_y(0)
            low_y(0)
            max_w(1)
            low_w(0)
            scale_w(1)
            max_w(2)
            low_w(1)
            scale_w(2)
            def low_phases(v):
                return v.rearrange("p (j q) -> p j q", q=PH)[:, :, 0:PH - PAD]

            def high_phases(v):
                return v.rearrange("p (j q) -> p j q", q=PH)[:, :, PH - PAD:PH]

            phases = low_phases, high_phases

            def x1_of(view, j0, nj):
                q, j0 = (slice(PAD, PH), j0) if view is low_phases else (slice(0, PAD), j0 + 1)
                return x1[:, q, j0:j0 + nj].rearrange("p q j -> p j q")

            dve.wait_ge(s_gs, 4)

            def step(i, proj, attn, tail, more):
                first = isinstance(i, int) and i == 0
                if isinstance(i, int) and i == 1:
                    low_w(6)
                    scale_w(7)
                if proj:
                    rotate(i, 0)
                if first:
                    max_w(3)
                    low_w(2)
                    scale_w(3)
                if attn:
                    keys(i, 0)
                if proj:
                    rotate(i, 1)
                if first:
                    max_w(4)
                    low_w(3)
                    scale_w(4)
                if attn:
                    mask_max(i, 0)
                    keys(i, 1)
                    if not proj:
                        mask_max(i, 1)
                        sums(i, 0)
                if tail:
                    dve.wait_ge(S["conv_ready"], i - 1)
                    dve.wait_ge(s_cb, 16 * (i - 1))
                    dve.tensor_tensor(cT.rearrange("p q (b o) -> p q b o", o=GC),
                                      CC.rearrange("p a (b q o) -> p q (a b) o", q=PH, o=GC),
                                      cbias.rearrange("p (b o) -> p b o", o=GC).unsqueeze(1).to_broadcast([P, PH, NG, GC]),
                                      ALU.add).then_inc(S["cT_ready"], 1)
                if attn and proj:
                    sums(i, 0)
                if proj:
                    rotate(i, 2)
                if first:
                    max_w(5)
                    low_w(4)
                    scale_w(5)
                if attn and proj:
                    mask_max(i, 1)
                if tail:
                    dve.wait_ge(S["low_ready"], i - 1)
                    dve.tensor_tensor(fs[:, 4:4 + EX], CC[:, 0, LOW:LOW + EX], brb[:, :], ALU.add
                                      ).then_inc(S["router_sum0"], 1)
                    dve.wait_ge(S["router_sum0"], i - 1)
                    dve.tensor_reduce(fs[:, 0:1], fs[:, 4:4 + EX], AX, ALU.max, negate=True
                                      ).then_inc(S["router_max"], 1)
                if attn:
                    sums(i, 1)
                if tail:
                    dve.wait_ge(S["router_exp"], i - 1)
                    dve.reciprocal(fs[:, 2:3], fs[:, 1:2]).then_inc(S["router_sum"], 1)
                    dve.wait_ge(S["router_sum"], i - 1)
                    dve.tensor_scalar(fs[:, 4 + 2 * EX:4 + 3 * EX], fs[:, 4 + EX:4 + 2 * EX], fs[:, 2:3], FFN_SCALE,
                                      ALU.mult, ALU.mult).then_inc(S["router_w"], 1)
                    dve.wait_ge(S["router_w"], i - 1)
                    dve.tensor_tensor(lows[:, :].rearrange("p (e r) -> p e r", r=R),
                                      CC[:, 0, 0:LOW].rearrange("p (e r) -> p e r", r=R),
                                      fs[:, 4 + 2 * EX:4 + 3 * EX].unsqueeze(2).to_broadcast([P, EX, R]), ALU.mult
                                      ).then_inc(S["lows_ready"], 1)
                if proj:
                    rotate(i, 3)
                if first:
                    mixed(1)
                    max_w(6)
                    low_w(5)
                    scale_w(6)
                if attn:
                    dve.wait_ge(S["pT0_ready"], i)
                    dve.tensor_copy(pT[:, 4:8, :], B[:, 1, :].rearrange("p (m t) -> p m t", m=4)
                                    ).then_inc(S["pT0_dve"], 1)
                if tail:
                    dve.wait_ge(S["f_ready"], i - 1)
                    if not (isinstance(i, int) and i == 2):
                        dve.wait_ge(s_out, 16 * (i - 2))
                    f = CC.rearrange("p a c -> p (a c)")
                    for view in phases:
                        ins = dve.tensor_tensor(view(res), view(f), x1_of(view, 0, D // PH), ALU.add)
                    ins.then_inc(S["result_ready"], 1)
                if attn:
                    dve.wait_ge(S["pT1_ready"], i)
                    dve.tensor_copy(pT[:, 12:16, :], B[:, 3, :].rearrange("p (m t) -> p m t", m=4)
                                    ).then_inc(S["pT1_dve"], 1)
                if isinstance(i, int) and i == 1:
                    low_w(7)
                if more and not first:
                    mixed(i + 1)
                if attn:
                    dve.wait_ge(S["o_high_ready"], i)
                    dve.scalar_tensor_tensor(oT[:, 1, :, :], CC.rearrange("p a (c t) -> p (a c) t", c=4), o_s,
                                             oT[:, 0, :, :], ALU.mult, ALU.subtract).then_inc(S["oT_ready"], 1)
                if proj:
                    values(i, 0)
                if more:
                    scale_y(i + 1)
                if proj:
                    values(i, 1)
                if more:
                    low_y(i + 1)
                if first:
                    max_w(7)
                if proj:
                    scale_o(i)
                if attn:
                    dve.wait_ge(s_res, 16 * i)
                    dve.wait_ge(S["op_ready"], i)
                    for n in range(2):
                        dve.wait_ge(s_wo[n], i)
                        at = slice(n * BLK, (n + 1) * BLK)
                        for view in phases:
                            ins = dve.scalar_tensor_tensor(x1_of(view, n * BLK // PH, BLK // PH), view(A[n]), op[:, n:n + 1],
                                                           view(xres[:, at]), ALU.mult, ALU.add)
                        ins.then_inc(S["x1a_ready" if n == 0 else "x1b_ready"], 1)
            steps(dve, step)


LATE_AT = tuple(np.cumsum([0, NG * PW, D, D, GROUPS * SHIFTS * P]).tolist())
LATE = max(LATE_AT[-1], WCOL)
V_ATT, V_ATTT, V_MIX0, V_BIAS = 4, 6, 17, 18
A_CTX, A_MIX = 2, 4
PE_MIX = 8


def kernel(**inputs):
    import numpy as np
    import concourse.bacc as _bacc
    from concourse import mybir as _mybir
    from concourse.bass_utils import run_bass_kernel_spmd as _run

    g = {k: np.asarray(v) for k, v in inputs.items()}

    def c(a):
        return np.ascontiguousarray(a)

    wt = g["L0_cond2_weight"]
    toep = np.zeros((GC, PH, GROUPS, SHIFTS, PH, GC), wt.dtype)
    for gp in range(GROUPS):
        for ph in range(PH):
            for q in range(PH):
                for d in range(SHIFTS):
                    k = PH * d + ph - q
                    if 0 <= k < TAPS:
                        toep[:, ph, gp, d, q, :] = wt[gp * GC:(gp + 1) * GC, :, k].T
    t = np.arange(T, dtype=np.float32)
    pack = np.zeros((P, PACKED), np.float32)
    mixk = g["L0_cond_weight"].reshape(KMIX, T, T)
    for name, a in (("W0", g["L0_cond_W0"]), ("W1", g["L0_cond_W1"]), ("W2", g["L0_cond_W2"]),
                    ("b0", g["L0_cond_b0"][:, None]), ("b1", g["L0_cond_b1"][:, None]),
                    ("cw", g["L0_cond2_c_weight"].T), ("cond", g["cond_128"].T),
                    ("mix", np.tile(mixk.transpose(2, 0, 1).reshape(T, KMIX * T), (2, 1))),
                    ("halves", np.arange(NB)[:, None] == np.arange(P)[None, :] // T), ("bias_k", g["L0_cond_bias_k"]), ("b2", g["L0_cond_b2"][None]), ("fside", g["fside_S_0"][None]),
                    ("br", g["L0_ffn_br"][None])):
        pack[:a.shape[0], PACK[name]] = a
    arrays = {
        "x": c(g["x"].reshape(NB * T, D)),
        "pack": pack,
        "shapes": np.concatenate([
            np.eye(P, dtype=np.float32), np.tile(np.triu(np.full((T, T), NEG, np.float32), 1), (2, 1)),
            np.tile(np.stack([np.cos(t), np.sin(t)], 1), (2, 1)).astype(np.float32)], 1),
        "mixk": c(mixk.transpose(0, 2, 1).reshape(KMIX, T * T)),
        "wqkvoT": c(np.stack([g["L0_attn_wq"].T, g["L0_attn_wk"].T, g["L0_attn_wv"].T, g["L0_attn_wo"].T])),
        "toep": toep.reshape(P, GROUPS, SHIFTS, P),
        "abT": c(np.concatenate([g["L0_ffn_A"].reshape(LOW, D), g["L0_ffn_Wr"]]).T),
        "bmT": c(g["L0_ffn_B"].transpose(0, 2, 1).reshape(LOW, D)),
    }
    nc = _bacc.Bacc("TRN2", target_bir_lowering=False, num_devices=1, dynamic_dma_scratch_size=1024)
    args = {k: nc.dram_tensor(k + "_dram", a.shape, _mybir.dt.from_np(a.dtype), kind="ExternalInput").ap()
            for k, a in arrays.items()}
    out = nc.dram_tensor("out_dram", (NB * T, D), F32, kind="ExternalOutput").ap()
    build(nc, **args, out=out)
    r = _run(nc, [{k + "_dram": a for k, a in arrays.items()}], core_ids=[0])
    return r.results[0]["out_dram"].reshape(NB, T, D)
```

```python
from contextlib import ExitStack

import concourse.bass as bass
from concourse import mybir
import numpy as np

F32 = mybir.dt.float32
F16 = mybir.dt.float16
U32 = mybir.dt.uint32
ALU = mybir.AluOpType
ACT = mybir.ActivationFunctionType
AX = mybir.AxisListType.X

P = 128
NB = 32
T = 64
D = 1024
NP = NB // 2
NH, HD = 32, 32
C = D // P
BLK = 512
NM = NH // 2
KMIX = 8
HID = 128
TAPS, GROUPS = 9, 4
PH = 8
GC = P // PH
NG = P // GC
SHIFTS = 2
PAD = TAPS // 2
PW = D // PH + 1
EX, R = 8, 16
LOW = EX * R
FFN_SCALE = EX * 32.0 / 16.0
NEG = -1e30
NW = 4 * D // BLK
WCOL = C * BLK
EXPO = 0x7F800000
TINY = 2.0 ** -100
TOP = 2.0 ** -13


PACK = {}
for _name, _width in (("W0", HID), ("W1", HID), ("W2", KMIX), ("b0", 1), ("b1", 1), ("cw", T), ("cond", NB),
                      ("mix", KMIX * T), ("halves", P), ("bias_k", T), ("b2", KMIX), ("fside", T),
                      ("br", EX)):
    _at = max((v.stop for v in PACK.values()), default=0)
    PACK[_name] = slice(_at, _at + _width)
PACKED = PACK["br"].stop


def build(nc, x, pack, shapes, mixk, wqkvoT, toep, abT, bmT, out):
    SCALE = float(HD) ** -0.5
    ctx = ExitStack()
    with ctx:
        def sb(name, shape):
            return ctx.enter_context(nc.sbuf_tensor(name, shape, F32))

        def sem(name):
            return ctx.enter_context(nc.semaphore(name))

        arena = sb("arena", [P, NW * WCOL + LATE])
        w = arena[:, 0:NW * WCOL].bitcast(F16).rearrange("p (n h c k) -> p n h c k", n=NW, h=2, c=C)
        xrep, xres, res, toe = (arena[:, NW * WCOL + a:NW * WCOL + b] for a, b in zip(LATE_AT, LATE_AT[1:]))
        xrep = xrep.rearrange("p (b j) -> p b j", b=NG)
        toe = toe.rearrange("p (g d n) -> p g d n", g=GROUPS, d=SHIFTS)

        def raw(n):
            return arena[:, (n + 1) * WCOL:(n + 2) * WCOL].rearrange("p (c k) -> p c k", c=C)

        ab = sb("ab", [P, PH, LOW + EX])
        bm = sb("bm", [P, D])
        kc = sb("kc", [P, P + T + 2])
        idn, mask, cs = kc[:, 0:P], kc[:, P:P + T], kc[:, P + T:P + T + 2]
        brb = sb("brb", [P, EX])
        xy = sb("xy", [P, D])
        mixw = sb("mixw", [P, 2 * P])
        cbias = sb("cbias", [P, P])
        yT = ctx.enter_context(nc.sbuf_tensor("yT", [P, 2, C, P], F16))
        rs = sb("rs", [P, 2, BLK])
        qr = sb("qr", [P, D])
        kr = sb("kr", [P, D])
        qoT = sb("qoT", [P, C, P])
        kbd = sb("kbd", [P, 4, 2, 4, T])
        sm = sb("sm", [P, 2, NH // 2, T])
        stat = sb("stat", [P, 2, 3, NH // 2])
        pT = sb("pT", [P, NM, P])
        vbd = sb("vbd", [P, 2, NM, 2, HD])
        x1 = sb("x1", [P, PH, PW])
        cT = sb("cT", [P, PH, P])
        fs = sb("fs", [P, 4 + 3 * EX])
        lows = sb("lows", [P, P])
        sc = sb("sc", [P, 34])
        rotw, vw, ow = sc[:, 0:8], sc[:, 8:10], sc[:, 10:12]
        y_max, y_all, y_c, y_s, y_h = (sc[:, k:k + 1] for k in range(12, 17))
        rotp, vp = sc[:, 17:25], sc[:, 25:27]
        v_max, v_all, v_c, o_s, o_h = (sc[:, k:k + 1] for k in range(27, 32))
        op = sc[:, 32:34]
        oT = qoT[:, :, :].rearrange("p c t -> p (c t)").bitcast(F16).rearrange("p (h c t) -> p h c t", h=2, c=C)
        y32 = rs[:, :, :].rearrange("p a k -> p (a k)")
        w_max, w_all, w_c, w_s = (lows[:, 96 + 8 * k:104 + 8 * k] for k in range(4))
        x1_last = sm.rearrange("p a h k -> p (a h k)")[:, 0:PH * PW].rearrange("p (q j) -> p q j", q=PH)
        yT_second = cT.rearrange("p q t -> p (q t)").bitcast(F16).rearrange("p (h c t) -> p h c t", h=2, c=C)
        xrep_last = arena[:, 0:NG * PW].rearrange("p (b j) -> p b j", b=NG)
        q_last = arena[:, NG * PW:NG * PW + D].rearrange("p (c t) -> p c t", c=C)
        kbd_last = arena[:, WCOL:WCOL + 4 * 2 * 4 * T].rearrange("p (c b r k) -> p c b r k", c=4, b=2, r=4)
        cT_last = qr.rearrange("p (q t) -> p q t", q=PH)

        ps = ctx.enter_context(nc.psum_tensor("ps", [P, 8, BLK], F32))
        A = [ps[:, 0, :], ps[:, 1, :]]
        B = ps[:, 2:6, :]
        CC = ps[:, 6:8, :]

        mixd = nc.dram_tensor("mixd", [NP, P, T], F32, kind="Internal").ap()
        biasd = nc.dram_tensor("biasd", [2, NB * T], F32, kind="Internal").ap()

        s_small = sem("small_loaded")
        s_const = sem("const_loaded")
        s_w = [sem(f"w{n}_loaded") for n in range(8)]
        s_mixk = sem("mix_kernels_loaded")
        s_xy = sem("xy_loaded")
        s_cb = sem("cbias_loaded")
        s_res = sem("residual_loaded")
        s_rep = [sem(f"xrep{h}_turned") for h in range(2)]
        s_out = sem("out_stored")
        s_pb = sem("pair_biases_stored")
        s_pm = sem("pair_mixing_stored")
        s_ps = sem("setup_pe")
        s_vs = sem("setup_dve")
        s_as = sem("setup_act")
        s_gs = sem("setup_pool")
        s_wmax, s_wc, s_ws, s_wh, s_whi, s_wlo0, s_wlo1, s_wconst, s_wsc = (sem("w_" + k) for k in (
            "max_ready", "max_shared", "scale_ready", "inverse_ready", "high_ready", "low_pool_ready",
            "low_dve_ready", "consts_ready", "scaled"))
        s_wall = sem("w_all_ready")
        s_first = sem("first_rotp_ready")
        names = """y_ready yT_ready qT_ready qT_moved k0_ready k1_ready
            s0_ready s1_ready conv_ready cT_ready low_ready router_max router_exp router_sum lows_ready
            lowT_ready lowT_moved f_ready result_ready pT0_turned pT1_turned pT0_act pT1_act pT0_ready pT1_ready
            pv_ready oT_ready v0_act v0_dve v1_act v1_dve x1a_ready x1b_ready
            masked0 masked1 max0 max1 shifted0 shifted1 exp0 exp1 sum0 sum1 recip0 recip1 probs0 probs1
            router_sum0 router_w
            y32_ready y_max_ready y_all_ready y_c_ready y_s_ready y_h_ready y_high_ready rotp_ready
            v_max_ready v_all_ready v_c_ready o_s_ready o_h_ready op_ready o_high_ready""".split()
        S = {n: sem(n) for n in names}
        s_g = [sem(f"g{n}_ready") for n in range(6)]
        s_sin = [sem(f"sin{n}_ready") for n in range(4)]
        s_rot = [sem(f"rot{n}_ready") for n in range(4)]
        s_wo = [sem(f"wo{n}_ready") for n in range(2)]

        block = ctx.enter_context(nc.Block())

        def steps(eng, step, finish):
            step(0, True, False, False, True)
            step(1, True, True, False, True)
            step(2, True, True, True, True)
            with eng.Fori(3, NP - 1) as i:
                step(i, True, True, True, True)
            step(NP - 1, True, True, True, False)
            finish()

        hT = lows[:, 0:NB]
        h2T = lows[:, NB:2 * NB]
        small = kbd[:, :, :, :, :].rearrange("p c b r k -> p (c b r k)")

        def packed(name, rows=P):
            return small[0:rows, PACK[name]]

        w0_s, w1_s, w2_s, b0_s, b1_s = (packed(k) for k in ("W0", "W1", "W2", "b0", "b1"))
        cw_s, cond = packed("cw"), packed("cond")
        b2_s, fside_s, br_s = (packed(k, 1) for k in ("b2", "fside", "br"))
        bk_s = packed("bias_k", KMIX)
        mix_s, halves_s = packed("mix"), packed("halves", NB)
        att = small[0:NB, 1200:1200 + KMIX]
        st_s = small[0:NB, 1208:1212]
        attT = small[0:KMIX, 1216:1216 + NB]
        attT0 = small[0:KMIX, 1248:1248 + 2 * P].rearrange("k (h m) -> k h m", h=2)
        att0 = small[:, 1504:1504 + KMIX]
        acc0 = small[:, 1512:1512 + T]
        biases = small[0:NB, 1576:1576 + 2 * T].rearrange("p (a t) -> p a t", a=2)
        ones = small[:, 1704:1704 + P]
        mixk_s = arena[0:KMIX, NW * WCOL:NW * WCOL + T * T]
        mixed_k = [sm[0:NB, :, :, :].rearrange("p a h k -> p (a h k)"), pT[0:NB, :, :].rearrange("p m t -> p (m t)")]

        def bank(n):
            return ps[:, (4, 5, 6, 7, 1, 0, 2, 3)[n], :]

        def x1_at(i):
            return x1_last if isinstance(i, int) and i == NP else x1

        def queries_at(i):
            return q_last if isinstance(i, int) and i == NP else qoT

        def keys_at(i, s):
            return kbd_last if isinstance(i, int) and i == NP and s == 1 else kbd

        def ffn_banks(i):
            return B[:, 0:2, :] if isinstance(i, int) and i > NP else CC

        def cT_at(i):
            return cT_last if isinstance(i, int) and i > NP else cT

        def xrep_at(i):
            return xrep_last if isinstance(i, int) and i == NP else xrep

        def yT_at(p):
            return yT_second if isinstance(p, int) and p == 1 else yT

        def load_w(eng, n):
            eng.dma_start(raw(n), wqkvoT[n // 2].rearrange("(c p) n -> p c n", p=P)[:, :, n % 2 * BLK:(n % 2 + 1) * BLK]
                          ).then_inc(s_w[n], 16)

        @block.sync
        def _(sp):
            sp.dma_start(small[:, 0:PACKED], pack).then_inc(s_small, 16)
            sp.dma_start(kc[:, :], shapes).then_inc(s_small, 16)
            sp.dma_start(mixk_s, mixk).then_inc(s_mixk, 16)
            sp.dma_start(xy[:, :], x[0:P, :]).then_inc(s_xy, 16)
            sp.wait_ge(s_small, 32)
            load_w(sp, 0)
            load_w(sp, 1)

            def load_bias(k, p):
                return (mixw[:, P:2 * P] if k == 0 else cbias[:, :]), biasd[k, bass.ds(p * P, P)].partition_broadcast(P)

            sp.wait_ge(s_as, A_CTX)
            sp.wait_ge(s_vs, V_BIAS)
            sp.dma_start(biasd.rearrange("a (b t) -> b a t", t=T), biases).then_inc(s_pb, 16)
            load_w(sp, 2)
            load_w(sp, 3)
            for k in range(2):
                sp.wait_ge(s_as, A_MIX + 4 * k + 4)
                sp.dma_start(mixd.rearrange("n (h i) t -> (n h) (i t)", h=2)[:, k * T * T // 2:(k + 1) * T * T // 2],
                             mixed_k[k]).then_inc(s_pm, 16)
            load_w(sp, 4)

            def store(i):
                sp.wait_ge(S["result_ready"], i - 1)
                sp.dma_start(out[bass.ds((i - 2) * P, P), :], res[:, :]).then_inc(s_out, 16)

            def step(i, proj, attn, tail, more):
                if more:
                    first = isinstance(i, int) and i == 0
                    if first:
                        sp.wait_ge(s_pb, 16)
                        sp.wait_ge(s_pm, 32)
                    sp.wait_ge(S["y_ready"], i + 1)
                    sp.wait_ge(S["y32_ready"], i + 1)
                    sp.dma_start(xy[:, :], x[bass.ds((i + 1) * P, P), :]).then_inc(s_xy, 16)
                    for h in range(2):
                        sp.dma_start(mixw[h * T:(h + 1) * T, h * T:(h + 1) * T], mixd[i + 1, h * T:(h + 1) * T, :]
                                     ).then_inc(s_xy, 16)
                    sp.dma_start(*load_bias(0, i + 1)).then_inc(s_xy, 16)
                    if first:
                        sp.dma_start(*load_bias(1, 0)).then_inc(s_cb, 16)
                        for n in range(5, NW):
                            load_w(sp, n)
                        sp.dma_start(ab[:, :, :], abT.rearrange("(j q) n -> j q n", q=PH)).then_inc(s_const, 16)
                        sp.dma_start(bm[:, :], bmT).then_inc(s_const, 16)
                if isinstance(i, int) and i == 1:
                    sp.wait_ge(s_wlo0, NW)
                    sp.wait_ge(s_wlo1, NW)
                    sp.dma_start(toe[:, :, :, :], toep).then_inc(s_const, 16)
                if attn:
                    if tail:
                        sp.wait_ge(S["x1b_ready"], i - 1)
                    sp.dma_start(xres[:, :], x[bass.ds((i - 1) * P, P), :]).then_inc(s_res, 16)
                if tail:
                    sp.wait_ge(S["cT_ready"], i - 1)
                    sp.dma_start(*load_bias(1, i - 1)).then_inc(s_cb, 16)
                    if not (isinstance(i, int) and i == NP):
                        store(i)
                if attn:
                    sp.wait_ge(S["x1b_ready"], i)
                    if tail and not (isinstance(i, int) and i == NP):
                        sp.wait_ge(S["conv_ready"], i - 1)
                    for b in range(NG):
                        sp.dma_start(xrep_at(i)[:, b, :], x1_at(i)[b * GC:(b + 1) * GC, :, :]
                                     ).then_inc(s_rep[b // (NG // 2)], 16)

            def finish():
                step(NP, False, True, True, False)
                store(NP)
                store(NP + 1)

            steps(sp, step, finish)
            sp.wait_ge(s_out, 16 * NP)

        @block.gpsimd
        def _(pool):
            pool.memset(ones, 1.0).then_inc(s_gs, 1)
            pool.memset(mixw[:, 0:P], 0.0).then_inc(s_gs, 1)
            pool.memset(vbd[:, :, :, :, :], 0.0).then_inc(s_gs, 1)
            pool.memset(x1[:, 0:PAD, 0], 0.0)
            pool.memset(x1[:, PAD:PH, PW - 1], 0.0).then_inc(s_gs, 1)

            def alone():
                pool.wait_ge(s_gs, 4)

            def share(dst_all, dst_c, src, all_ready, c_ready, k):
                pool.partition_all_reduce(dst_all, src, P, bass.bass_isa.ReduceOp.max).then_inc(all_ready, 1)
                alone()
                pool.wait_ge(all_ready, k)
                pool.tensor_scalar(dst_c, dst_all, TINY, TOP, ALU.max, ALU.mult).then_inc(c_ready, 1)

            def share_w(n):
                alone()
                pool.wait_ge(s_wmax, n + 1)
                share(w_all[:, n:n + 1], w_c[:, n:n + 1], w_max[:, n:n + 1], s_wall, s_wc, n + 1)

            def w_consts(n):
                pool.wait_ge(s_wh, n + 1)
                h = w_c[:, n:n + 1]
                if n < 4:
                    pool.tensor_scalar(rotw[:, 2 * n:2 * n + 2], cs[:, :], h, 0.25, ALU.mult, ALU.mult).then_inc(s_wconst, 1)
                else:
                    dst = vw if n < 6 else ow
                    pool.tensor_scalar(dst[:, n % 2:n % 2 + 1], h, 0.25, None, ALU.mult).then_inc(s_wconst, 1)


            def share_y(own):
                alone()
                pool.wait_ge(S["y_max_ready"], own)
                share(y_all, y_c, y_max, S["y_all_ready"], S["y_c_ready"], own)

            def pair_consts(own, last):
                alone()
                pool.wait_ge(S["y_h_ready"], own)
                pool.wait_ge(S["v1_act"], last)
                pool.wait_ge(S["v1_dve"], last)
                pool.tensor_scalar(sc[:, 17:27], sc[:, 0:10], y_h, None, ALU.mult).then_inc(S["rotp_ready"], 1)

            def share_v(own):
                alone()
                pool.wait_ge(S["v_max_ready"], own)
                share(v_all, v_c, v_max, S["v_all_ready"], S["v_c_ready"], own)

            def out_consts(own, last):
                alone()
                pool.wait_ge(S["o_h_ready"], own)
                if last is not None:
                    pool.wait_ge(S["x1b_ready"], last)
                pool.tensor_scalar(op, ow, o_h, None, ALU.mult).then_inc(S["op_ready"], 1)

            def half(s, i):
                pool.wait_ge(S[f"masked{s}"], i)
                pool.wait_ge(S[f"max{s}"], i)
                pool.tensor_tensor(sm[:, s, :, :], sm[:, s, :, :],
                                   stat[:, s, 0, :].unsqueeze(2).to_broadcast([P, NH // 2, T]),
                                   ALU.subtract).then_inc(S[f"shifted{s}"], 1)

            def norm(s, i):
                pool.wait_ge(S[f"recip{s}"], i)
                pool.wait_ge(S[f"exp{s}"], i)
                pool.tensor_tensor(sm[:, s, :, :], sm[:, s, :, :],
                                   stat[:, s, 2, :].unsqueeze(2).to_broadcast([P, NH // 2, T]),
                                   ALU.mult).then_inc(S[f"probs{s}"], 1)

            def low_w(n):
                pool.wait_ge(s_whi, 2 * n + 1)
                if n:
                    pool.wait_ge(s_wlo1, n)
                cc = slice(0, C // 2)
                pool.tensor_tensor(w[:, n, 1, cc, :], raw(n)[:, cc, :], w[:, n, 0, cc, :], ALU.subtract
                                   ).then_inc(s_wlo0, 1)

            def first_consts(n):
                pool.wait_ge(S["y_h_ready"], 1)
                pool.wait_ge(s_wconst, n + 1)
                k = slice(2 * n, 2 * n + 2) if n < 4 else slice(4 + n, 5 + n)
                pool.tensor_scalar(sc[:, 17:27][:, k], sc[:, 0:10][:, k], y_h, None, ALU.mult).then_inc(s_first, 1)

            share_w(0)
            w_consts(0)
            share_w(1)
            share_y(1)
            low_w(0)
            w_consts(1)
            first_consts(0)
            first_consts(1)
            low_w(1)
            for n in range(2, 6):
                share_w(n)
                if n > 2:
                    low_w(n - 1)
                w_consts(n)
                first_consts(n)

            def step(i, proj, attn, tail, more):
                if isinstance(i, int) and i == 0:
                    share_w(6)
                    low_w(5)
                    w_consts(6)
                    share_y(2)
                    low_w(6)
                last, own, ahead = (c if isinstance(i, int) else pool.snap(pool.to_reg(c)) for c in (i - 1, i + 1, i + 2))
                if isinstance(i, int) and i == NP - 1:
                    pool.wait_ge(s_g[1], NP)
                    pool.memset(kbd_last[:, :, :, :, :], 0.0).then_inc(s_gs, 1)
                if attn:
                    if isinstance(i, int) and i == 1:
                        share_w(7)
                        w_consts(7)
                        pool.wait_ge(s_wconst, NW)
                    out_consts(i, last if tail else None)
                    half(0, i)
                    norm(0, i)
                    half(1, i)
                    norm(1, i)
                if isinstance(i, int) and i == 1:
                    low_w(7)
                if more:
                    if not (isinstance(i, int) and i == 0):
                        share_y(ahead)
                    pair_consts(ahead, own)
                if isinstance(i, int) and i == 0:
                    pool.wait_ge(s_ps, PE_MIX)
                    pool.wait_ge(s_pb, 16)
                    pool.memset(kbd[:, :, :, :, :], 0.0).then_inc(s_gs, 1)
                if proj and not (isinstance(i, int) and i == NP - 1):
                    share_v(own)

            def finish():
                half(0, NP)
                half(1, NP)
                norm(0, NP)
                norm(1, NP)
                share_v(NP)
                out_consts(NP, NP - 1)
                pool.wait_ge(S["pT1_turned"], NP)
                pool.memset(x1_last[:, 0:PAD, 0], 0.0)
                pool.memset(x1_last[:, PAD:PH, PW - 1], 0.0).then_inc(s_gs, 1)

            steps(pool, step, finish)

        @block.tensor
        def _(pe):
            pe.wait_ge(s_small, 32)
            pe.matmul(A[0][:, 0:NB], w0_s, cond, start=True, stop=True).then_inc(s_ps, 1)
            pe.wait_ge(s_gs, 1)
            pe.matmul(B[0:NB, 1, 0:T], cond, cw_s, start=True, stop=False)
            pe.matmul(B[0:NB, 1, 0:T], ones[0:1, 0:NB], fside_s, start=False, stop=True).then_inc(s_ps, 1)
            pe.matmul(B[:, 2, 0:EX], ones[0:1, :], br_s, start=True, stop=True).then_inc(s_ps, 1)
            pe.wait_ge(s_as, 1)
            pe.matmul(A[1][:, 0:NB], w1_s, hT, start=True, stop=True).then_inc(s_ps, 1)
            pe.wait_ge(s_as, 3)
            pe.matmul(B[0:NB, 0, 0:KMIX], h2T, w2_s, start=True, stop=False)
            pe.matmul(B[0:NB, 0, 0:KMIX], ones[0:1, 0:NB], b2_s, start=False, stop=True).then_inc(s_ps, 1)
            pe.wait_ge(s_vs, V_ATT)
            pe.transpose(B[0:KMIX, 3, 0:NB], att, idn[0:NB, 0:NB]).then_inc(s_ps, 1)
            pe.matmul(A[1][:, 0:KMIX], halves_s, att, start=True, stop=True).then_inc(s_ps, 1)
            pe.wait_ge(s_vs, V_ATTT)
            pe.matmul(A[0][0:NB, 0:T], attT, bk_s, start=True, stop=True)
            for h in range(2):
                mm = pe.matmul(A[0][:, (h + 1) * T:(h + 2) * T], attT0[:, h, :], bk_s, start=True, stop=True)
            mm.then_inc(s_ps, 1)

            def mix(p):
                pe.wait_ge(s_xy, 64 * p + 16)
                for c in range(C):
                    mm = pe.matmul(B[:, c // 4, c % 4 * P:(c % 4 + 1) * P], xy[:, c * P:(c + 1) * P], mixw[:, 0:P],
                                   start=True, stop=True)
                mm.then_inc(S["y_ready"], 1)

            def proj_block(i, n, between=None):
                if isinstance(i, int) and i == 0:
                    pe.wait_ge(s_as, A_MIX + 8)
                    pe.wait_ge(s_wlo0, n + 1)
                    pe.wait_ge(s_wlo1, n + 1)
                split_matmul(A[n % 2], yT_at(i), n, between).then_inc(s_g[n], 1)

            def split_matmul(o, v, n, between=None):
                for c in range(C):
                    if between and c == 3:
                        between()
                    pe.matmul(o, v[:, 0, c, :], w[:, n, 0, c, :], start=(c == 0), stop=False)
                    pe.matmul(o, v[:, 0, c, :], w[:, n, 1, c, :], start=False, stop=False)
                    mm = pe.matmul(o, v[:, 1, c, :], w[:, n, 0, c, :], start=False, stop=(c == C - 1))
                return mm

            def mixed_kernels(n):
                pe.matmul(bank(n)[0:NB, :], attT, mixk_s[:, n * BLK:(n + 1) * BLK], start=True, stop=True
                          ).then_inc(s_ps, 1)

            pe.wait_ge(s_mixk, 16)
            for n in range(2):
                mixed_kernels(n)
            pe.wait_ge(s_vs, V_MIX0)
            mix(0)
            for n in range(2, 8):
                if n == 4:
                    pe.wait_ge(s_vs, V_BIAS + 1)
                if n == 6:
                    pe.wait_ge(S["y32_ready"], 1)
                mixed_kernels(n)
            def turn_queries(i):
                pe.wait_ge(s_rot[0], i)
                pe.wait_ge(s_rot[1], i)
                for c in range(C):
                    mm = pe.transpose(B[:, c // 4, c % 4 * P:(c % 4 + 1) * P], qr[:, c * P:(c + 1) * P], idn[:, :])
                mm.then_inc(S["qT_ready"], 1)

            def scores(i, s):
                if s == 0:
                    pe.wait_ge(S["qT_moved"], i)
                pe.wait_ge(S[f"k{s}_ready"], i)
                for c in range(4):
                    for b in range(2):
                        o = B[b * T:(b + 1) * T, 2 * s + c // 2, c % 2 * 256:(c % 2 + 1) * 256]
                        mm = pe.matmul(o, queries_at(i)[:, 4 * s + c, b * T:(b + 1) * T],
                                       keys_at(i, s)[:, c, b, :, :].rearrange("p r k -> p (r k)"), start=True, stop=True)
                mm.then_inc(S[f"s{s}_ready"], 1)

            def turn_probs(i, s):
                pe.wait_ge(S[f"probs{s}"], i)
                for m in range(8):
                    mm = pe.transpose(B[:, 2 * s + m // 4, m % 4 * P:(m % 4 + 1) * P],
                                      sm[:, s, 2 * m:2 * m + 2, :].rearrange("p h k -> p (h k)"), idn[:, :])
                mm.then_inc(S[f"pT{s}_turned"], 1)

            def attend(i, f_before):
                for k in ("pT0_ready", "v0_act", "v0_dve", "v1_act", "v1_dve"):
                    pe.wait_ge(S[k], i)
                if isinstance(i, int) and i == NP:
                    pe.wait_ge(S["pT0_act"], 1)
                if f_before:
                    pe.wait_ge(S["result_ready"], i - 1)
                for m in range(NM):
                    if m == NM // 2:
                        pe.wait_ge(S["pT1_ready"], i)
                        pe.wait_ge(S["pT1_act"], i)
                    for b in range(2):
                        col = m // 2 % 4 * P + b * T
                        mm = pe.matmul(CC[m % 2 * T:(m % 2 + 1) * T, m // 8, col:col + T],
                                       vbd[:, b, m, :, :].rearrange("p a d -> p (a d)"),
                                       pT[:, m, b * T:(b + 1) * T], start=True, stop=True)
                mm.then_inc(S["pv_ready"], 1)

            def convolve(i):
                if isinstance(i, int) and i == 2:
                    pe.wait_ge(s_const, 48)
                if isinstance(i, int) and i > NP:
                    pe.wait_ge(S["pT0_ready"], NP)
                else:
                    pe.wait_ge(S["oT_ready"], i if isinstance(i, int) and i == NP else i - 1)
                for b in range(NG):
                    if b % (NG // 2) == 0:
                        pe.wait_ge(s_rep[b // (NG // 2)], 16 * NG // 2 * (i - 1))
                    o = ffn_banks(i).rearrange("p a (b n) -> p (a b) n", n=P)[:, b, :]
                    for d in range(SHIFTS):
                        mm = pe.matmul(o, xrep_at(i - 1)[:, b, d:d + P], toe[:, b % GROUPS, d, :],
                                       start=(d == 0), stop=(d == SHIFTS - 1))
                mm.then_inc(S["conv_ready"], 1)

            def down(i):
                pe.wait_ge(S["cT_ready"], i - 1)
                for q in range(PH):
                    mm = pe.matmul(ffn_banks(i)[:, 0, 0:LOW + EX], cT_at(i)[:, q, :], ab[:, q, :], start=(q == 0),
                                   stop=(q == PH - 1))
                mm.then_inc(S["low_ready"], 1)

            def turn_low(i):
                pe.wait_ge(S["lows_ready"], i - 1)
                pe.transpose(ffn_banks(i)[:, 1, 0:P], lows[:, :], idn[:, :]).then_inc(S["lowT_ready"], 1)

            def up(i):
                pe.wait_ge(S["lowT_moved"], i - 1)
                for n in range(2):
                    mm = pe.matmul(ffn_banks(i)[:, n, :], cT_at(i)[:, 0, :], bm[:, n * BLK:(n + 1) * BLK], start=True, stop=True)
                mm.then_inc(S["f_ready"], 1)

            def output(n, readers):
                for k, count in readers:
                    pe.wait_ge(S[k], count)
                split_matmul(A[n], oT, 6 + n).then_inc(s_wo[n], 1)

            def step(i, proj, attn, tail, more):
                def attend_between():
                    attend(i, tail)

                if proj:
                    pe.wait_ge(S["yT_ready"], i + 1)
                    if isinstance(i, int) and i == 1:
                        pe.wait_ge(S["v0_act"], 1)
                        pe.wait_ge(S["v0_dve"], 1)
                    elif attn:
                        pe.wait_ge(S["x1a_ready"], i - 1)
                    proj_block(i, 0)
                if attn:
                    turn_queries(i)
                if proj:
                    if isinstance(i, int) and i == 1:
                        pe.wait_ge(S["v1_act"], 1)
                        pe.wait_ge(S["v1_dve"], 1)
                    elif attn:
                        pe.wait_ge(S["x1b_ready"], i - 1)
                    proj_block(i, 1)
                if attn:
                    scores(i, 0)
                if tail:
                    convolve(i)
                if proj:
                    pe.wait_ge(s_rot[0], i + 1)
                    proj_block(i, 2)
                if attn:
                    scores(i, 1)
                if tail:
                    down(i)
                if isinstance(i, int) and i == 0:
                    mix(1)
                if proj:
                    pe.wait_ge(s_rot[1], i + 1)
                    proj_block(i, 3)
                if proj:
                    pe.wait_ge(s_rot[2], i + 1)
                    proj_block(i, 4)
                if tail:
                    turn_low(i)
                if attn:
                    turn_probs(i, 1)
                if more and attn:
                    pe.wait_ge(S["masked0"], i)
                    mix(i + 1)
                if tail:
                    up(i)
                if isinstance(i, int) and i == NP - 1:
                    pe.wait_ge(S["masked0"], i)
                    turn_queries(NP)
                if proj:
                    pe.wait_ge(s_rot[3], i + 1)
                    proj_block(i, 5, attend_between if attn else None)
                if attn and not (isinstance(i, int) and i == NP - 1):
                    if isinstance(i, int) and i == 1:
                        pe.wait_ge(s_wlo0, NW)
                        pe.wait_ge(s_wlo1, NW)
                    pe.wait_ge(S["oT_ready"], i)
                    for n in range(2):
                        output(n, ((f"v{n}_act", i + 1), (f"v{n}_dve", i + 1)))

            def finish():
                scores(NP, 0)
                scores(NP, 1)
                pe.wait_ge(S["oT_ready"], NP - 1)
                for n in range(2):
                    output(n, ((f"v{n}_act", NP), (f"v{n}_dve", NP)))
                turn_probs(NP, 0)
                turn_probs(NP, 1)
                attend(NP, False)
                pe.wait_ge(S["oT_ready"], NP)
                output(0, (("x1a_ready", NP - 1),))
                output(1, (("x1b_ready", NP - 1),))
                convolve(NP)
                down(NP)
                turn_low(NP)
                convolve(NP + 1)
                up(NP)
                down(NP + 1)
                turn_low(NP + 1)
                up(NP + 1)

            steps(pe, step, finish)

        @block.scalar
        def _(act):
            act.wait_ge(s_small, 32)
            act.wait_ge(s_ps, 1)
            act.activation(hT, A[0][:, 0:NB], ACT.Gelu, bias=b0_s).then_inc(s_as, 1)
            act.wait_ge(s_ps, 2)
            act.copy(biases[:, 1, :], B[0:NB, 1, 0:T]).then_inc(s_as, 1)
            act.wait_ge(s_ps, 4)
            act.activation(h2T, A[1][:, 0:NB], ACT.Gelu, bias=b1_s).then_inc(s_as, 1)
            act.wait_ge(s_vs, 2)
            act.activation(att, B[0:NB, 0, 0:KMIX], ACT.Exp, bias=st_s[:, 0:1], accum_out=st_s[:, 1:2]).then_inc(s_as, 1)

            def mixed_kernels(n):
                act.wait_ge(s_ps, PE_MIX + n + 1)
                act.copy(mixed_k[n // 4][:, n % 4 * BLK:(n % 4 + 1) * BLK], bank(n)[0:NB, :]).then_inc(s_as, 1)

            def high_w(n):
                for h in range(2):
                    cc = slice(h * C // 2, (h + 1) * C // 2)
                    scale = w_s[:, n:n + 1]
                    if h == 0:
                        act.wait_ge(s_ws, n + 1)
                        act.activation(raw(n)[:, cc, :], raw(n)[:, cc, :], ACT.Copy, scale=scale).then_inc(s_wsc, 1)
                        act.wait_ge(s_wsc, n + 1)
                        scale = 1.0
                        if n:
                            act.wait_ge(s_wlo0, n)
                    act.activation(w[:, n, 0, cc, :], raw(n)[:, cc, :], ACT.Copy, scale=scale).then_inc(s_whi, 1)

            def high_y(p):
                act.wait_ge(S["y_s_ready"], p + 1)
                if not (isinstance(p, int) and p <= 1):
                    act.wait_ge(s_g[5], p)
                act.activation(yT_at(p)[:, 0, :, :].rearrange("p c t -> p (c t)"), y32, ACT.Copy, scale=y_s
                               ).then_inc(S["y_high_ready"], 1)

            for n in range(2):
                mixed_kernels(n)
            high_w(0)
            for n in range(2, 6):
                mixed_kernels(n)
            high_y(0)
            for n in range(6, 8):
                mixed_kernels(n)
            high_w(1)

            act.wait_ge(s_gs, 3)

            def sine(i, n):
                act.wait_ge(s_g[n], i + 1)
                if isinstance(i, int) and i == 0:
                    act.wait_ge(s_first, n + 1)
                else:
                    act.wait_ge(S["rotp_ready"], i)
                if n < 2:
                    act.wait_ge(S["yT_ready"], i + 1)
                else:
                    act.wait_ge(s_rot[n - 2], i + 1)
                act.activation(rs[:, n % 2, :], A[n % 2], ACT.Copy, scale=rotp[:, 2 * n + 1:2 * n + 2]
                               ).then_inc(s_sin[n], 1)

            def values(i, n):
                act.wait_ge(s_g[4 + n], i + 1)
                if isinstance(i, int) and i == 0:
                    act.wait_ge(s_first, 5 + n)
                v = A[n][0:T, :].rearrange("p (m a d) -> p m a d", a=2, d=HD)
                for a in range(2):
                    ins = act.activation(vbd[a * T:(a + 1) * T, 0, 8 * n:8 * n + 8, a, :], v[:, :, a, :], ACT.Copy,
                                         scale=vp[0:T, n:n + 1])
                ins.then_inc(S[f"v{n}_act"], 1)

            def expo(i, s):
                act.wait_ge(S[f"shifted{s}"], i)
                act.activation(sm[:, s, :, :], sm[:, s, :, :], ACT.Exp, scale=SCALE).then_inc(S[f"exp{s}"], 1)

            def queries(i):
                act.wait_ge(S["qT_ready"], i)
                act.copy(queries_at(i)[:, :, :], B[:, 0:2, :].rearrange("p a (c t) -> p (a c) t", c=4)
                         ).then_inc(S["qT_moved"], 1)

            def router_exp(i):
                act.wait_ge(S["router_max"], i - 1)
                act.activation(fs[:, 4 + EX:4 + 2 * EX], fs[:, 4:4 + EX], ACT.Exp, bias=fs[:, 0:1],
                               accum_out=fs[:, 1:2]).then_inc(S["router_exp"], 1)

            def move_low(i):
                act.wait_ge(S["lowT_ready"], i - 1)
                act.copy(cT_at(i)[:, 0, :], ffn_banks(i)[:, 1, 0:P]).then_inc(S["lowT_moved"], 1)

            def probs(i, s):
                act.wait_ge(S[f"pT{s}_turned"], i if s else 1)
                act.copy(pT[:, 8 * s:8 * s + 4, :], B[:, 2 * s, :].rearrange("p (m t) -> p m t", m=4)
                         ).then_inc(S[f"pT{s}_act"], 1)

            def high_o(i):
                act.wait_ge(S["pv_ready"], i)
                act.wait_ge(S["o_s_ready"], i)
                act.activation(oT[:, 0, :, :], CC.rearrange("p a (c t) -> p (a c) t", c=4), ACT.Copy, scale=o_s
                               ).then_inc(S["o_high_ready"], 1)

            def step(i, proj, attn, tail, more):
                first = isinstance(i, int) and i == 0
                if proj:
                    sine(i, 0)
                if first:
                    high_w(2)
                if attn:
                    queries(i)
                if proj:
                    sine(i, 1)
                if first:
                    high_w(3)
                    high_w(4)
                if attn:
                    expo(i, 0)
                if proj:
                    sine(i, 2)
                if isinstance(i, int) and i == 1:
                    high_w(7)
                if first:
                    high_w(5)
                if tail:
                    router_exp(i)
                if attn:
                    expo(i, 1)
                if proj:
                    sine(i, 3)
                if tail:
                    move_low(i)
                if attn:
                    probs(i, 1)
                    if isinstance(i, int) and i == NP - 1:
                        queries(NP)
                    high_o(i)
                if first:
                    high_w(6)
                    high_y(1)
                if proj:
                    values(i, 0)
                    values(i, 1)
                if more and not first:
                    high_y(i + 1)

            def finish():
                expo(NP, 0)
                expo(NP, 1)
                probs(NP, 0)
                probs(NP, 1)
                high_o(NP)
                for i in (NP, NP + 1):
                    router_exp(i)
                    move_low(i)

            steps(act, step, finish)

        @block.vector
        def _(dve):
            n = [0]

            def done(ins):
                n[0] += 1
                ins.then_inc(s_vs, 1)
                dve.wait_ge(s_vs, n[0])
                return n[0]

            def scales(s_out, h_out, c, s_ready, h_ready):
                dve.tensor_scalar(s_out.bitcast(U32), c.bitcast(U32), EXPO, EXPO, ALU.bitwise_and, ALU.bitwise_xor
                                  ).then_inc(s_ready, 1)
                return dve.tensor_scalar(h_out.bitcast(U32), c.bitcast(U32), EXPO, None, ALU.bitwise_and
                                         ).then_inc(h_ready, 1)

            def max_w(n):
                dve.wait_ge(s_w[n], 16)
                dve.tensor_reduce(w_max[:, n:n + 1], raw(n), mybir.AxisListType.XY, ALU.max, apply_absolute_value=True
                                  ).then_inc(s_wmax, 1)

            def scale_w(n):
                dve.wait_ge(s_wc, n + 1)
                scales(w_s[:, n:n + 1], w_c[:, n:n + 1], w_c[:, n:n + 1], s_ws, s_wh)

            def low_w(n):
                dve.wait_ge(s_whi, 2 * n + 2)
                if n:
                    dve.wait_ge(s_wlo1, n)
                cc = slice(C // 2, C)
                dve.scalar_tensor_tensor(w[:, n, 1, cc, :], raw(n)[:, cc, :], w_s[:, n:n + 1], w[:, n, 0, cc, :],
                                         ALU.mult, ALU.subtract).then_inc(s_wlo1, 1)

            dve.wait_ge(s_ps, 3)
            done(dve.tensor_copy(brb[:, :], B[:, 2, 0:EX]))
            dve.wait_ge(s_ps, 5)
            done(dve.tensor_reduce(st_s[:, 0:1], B[0:NB, 0, 0:KMIX], AX, ALU.max, negate=True))
            dve.wait_ge(s_as, 4)
            done(dve.reciprocal(st_s[:, 2:3], st_s[:, 1:2]))
            assert done(dve.tensor_scalar(att, att, st_s[:, 2:3], None, ALU.mult)) == V_ATT
            dve.wait_ge(s_ps, 6)
            assert done(dve.tensor_copy(attT, B[0:KMIX, 3, 0:NB])) == V_ATTT - 1
            assert done(dve.tensor_copy(attT0, attT[:, 0:2].unsqueeze(2).to_broadcast([KMIX, 2, P]))) == V_ATTT
            dve.wait_ge(s_ps, 7)
            done(dve.tensor_copy(att0, A[1][:, 0:KMIX]))
            done(dve.tensor_scalar(acc0, mix_s[:, 0:T], att0[:, 0:1], None, ALU.mult))
            for k in range(1, KMIX):
                done(dve.scalar_tensor_tensor(acc0, mix_s[:, k * T:(k + 1) * T], att0[:, k:k + 1], acc0, ALU.mult,
                                              ALU.add))
            dve.wait_ge(s_gs, 2)
            done(dve.tensor_copy(mixw[0:T, 0:T], acc0[0:T]))
            assert done(dve.tensor_copy(mixw[T:P, T:P], acc0[T:P])) == V_MIX0
            dve.wait_ge(s_ps, 8)
            assert done(dve.tensor_copy(biases[:, 0, :], A[0][0:NB, 0:T])) == V_BIAS
            done(dve.tensor_copy(mixw[:, P:2 * P], A[0][:, T:3 * T]))

            def mixed(p):
                dve.wait_ge(S["y_ready"], p + 1)
                if not (isinstance(p, int) and p == 0):
                    dve.wait_ge(s_rot[3], p)
                dve.tensor_tensor(y32.rearrange("p (c t) -> p c t", c=C), B[:, 0:2, :].rearrange("p a (c t) -> p (a c) t", c=4),
                                  mixw[:, P:2 * P].unsqueeze(1).to_broadcast([P, C, P]), ALU.add
                                  ).then_inc(S["y32_ready"], 1)
                dve.wait_ge(S["y32_ready"], p + 1)
                dve.tensor_reduce(y_max, y32, AX, ALU.max, apply_absolute_value=True).then_inc(S["y_max_ready"], 1)

            def scale_y(p):
                dve.wait_ge(S["y_c_ready"], p + 1)
                if not (isinstance(p, int) and p <= 1):
                    dve.wait_ge(S["rotp_ready"], p - 1)
                elif p == 1:
                    dve.wait_ge(s_first, 6)
                scales(y_s, y_h, y_c, S["y_s_ready"], S["y_h_ready"])

            def low_y(p):
                dve.wait_ge(S["y_high_ready"], p + 1)
                dve.scalar_tensor_tensor(yT_at(p)[:, 1, :, :].rearrange("p c t -> p (c t)"), y32, y_s,
                                         yT_at(p)[:, 0, :, :].rearrange("p c t -> p (c t)"), ALU.mult, ALU.subtract
                                         ).then_inc(S["yT_ready"], 1)

            def max_v(p):
                for k in ("v0_act", "v0_dve", "v1_act", "v1_dve"):
                    dve.wait_ge(S[k], p + 1)
                dve.tensor_reduce(v_max, vbd[:, :, :, :, :].rearrange("p b m a d -> p (b m a d)"), AX, ALU.max,
                                  apply_absolute_value=True).then_inc(S["v_max_ready"], 1)

            def scale_o(p):
                dve.wait_ge(S["v_c_ready"], p + 1)
                if not (isinstance(p, int) and p == 0):
                    dve.wait_ge(S["op_ready"], p)
                scales(o_s, o_h, v_c, S["o_s_ready"], S["o_h_ready"])

            def rotate(i, n):
                dve.wait_ge(s_sin[n], i + 1)
                if attn_of(i):
                    dve.wait_ge(S[("qT_ready", "qT_ready", "k0_ready", "k1_ready")[n]], i)
                a = A[n % 2].rearrange("p (f e) -> p f e", e=2)
                t = rs[:, n % 2, :].rearrange("p (f e) -> p f e", e=2)
                o = (qr if n < 2 else kr)[:, n % 2 * BLK:(n % 2 + 1) * BLK].rearrange("p (f e) -> p f e", e=2)
                cos = rotp[:, 2 * n:2 * n + 1]
                dve.scalar_tensor_tensor(o[:, :, 0], a[:, :, 0], cos, t[:, :, 1], ALU.mult, ALU.subtract)
                dve.scalar_tensor_tensor(o[:, :, 1], a[:, :, 1], cos, t[:, :, 0], ALU.mult, ALU.add
                                         ).then_inc(s_rot[n], 1)

            def attn_of(i):
                return not (isinstance(i, int) and i == 0)

            def keys(i, s):
                dve.wait_ge(s_rot[2 + s], i)
                if isinstance(i, int) and i == 1:
                    dve.wait_ge(s_gs, 5)
                if isinstance(i, int) and i == NP and s == 1:
                    dve.wait_ge(s_gs, 6)
                elif s == 1:
                    dve.wait_ge(S["s0_ready"], i)
                elif not (isinstance(i, int) and i == 1):
                    dve.wait_ge(S["s1_ready"], i - 1)
                heads = kr[:, s * BLK:(s + 1) * BLK].rearrange("p (c r f) -> p c r f", r=4, f=HD)
                for a in range(4):
                    for r in range(4):
                        ins = dve.transpose(keys_at(i, s)[r * HD:(r + 1) * HD, :, a // 2, r, a % 2 * 32:(a % 2 + 1) * 32],
                                            heads[a * 32:(a + 1) * 32, :, r, :])
                ins.then_inc(S[f"k{s}_ready"], 1)

            def values(i, n):
                dve.wait_ge(s_g[4 + n], i + 1)
                if isinstance(i, int) and i == 0:
                    dve.wait_ge(s_first, 5 + n)
                v = A[n][T:P, :].rearrange("p (m a d) -> p m a d", a=2, d=HD)
                for a in range(2):
                    ins = dve.tensor_scalar(vbd[a * T:(a + 1) * T, 1, 8 * n:8 * n + 8, a, :], v[:, :, a, :],
                                            vp[T:P, n:n + 1], None, ALU.mult)
                ins.then_inc(S[f"v{n}_dve"], 1)

            def mask_max(i, s):
                dve.wait_ge(S[f"s{s}_ready"], i)
                dve.tensor_tensor(sm[:, s, :, :], B[:, 2 * s:2 * s + 2, :].rearrange("p a (h k) -> p (a h) k", k=T),
                                  mask[:, :].unsqueeze(1).to_broadcast([P, NH // 2, T]), ALU.add
                                  ).then_inc(S[f"masked{s}"], 1)
                dve.wait_ge(S[f"masked{s}"], i)
                dve.tensor_reduce(stat[:, s, 0, :], sm[:, s, :, :], AX, ALU.max).then_inc(S[f"max{s}"], 1)

            def sums(i, s):
                dve.wait_ge(S[f"exp{s}"], i)
                dve.tensor_reduce(stat[:, s, 1, :], sm[:, s, :, :], AX, ALU.add).then_inc(S[f"sum{s}"], 1)
                dve.wait_ge(S[f"sum{s}"], i)
                dve.reciprocal(stat[:, s, 2, :], stat[:, s, 1, :]).then_inc(S[f"recip{s}"], 1)

            max_w(0)
            scale_w(0)
            max_w(1)
            mixed(0)
            scale_w(1)
            low_w(0)
            scale_y(0)
            low_y(0)
            max_w(2)
            low_w(1)
            scale_w(2)
            max_w(3)
            scale_w(3)
            max_w(4)
            low_w(2)
            scale_w(4)
            def low_phases(v):
                return v.rearrange("p (j q) -> p j q", q=PH)[:, :, 0:PH - PAD]

            def high_phases(v):
                return v.rearrange("p (j q) -> p j q", q=PH)[:, :, PH - PAD:PH]

            phases = low_phases, high_phases

            def x1_of(x1, view, j0, nj):
                q, j0 = (slice(PAD, PH), j0) if view is low_phases else (slice(0, PAD), j0 + 1)
                return x1[:, q, j0:j0 + nj].rearrange("p q j -> p j q")

            dve.wait_ge(s_gs, 4)

            def conv_bias(i):
                dve.wait_ge(S["conv_ready"], i - 1)
                dve.wait_ge(s_cb, 16 * (i - 1))
                dve.tensor_tensor(cT_at(i).rearrange("p q (b o) -> p q b o", o=GC),
                                  ffn_banks(i).rearrange("p a (b q o) -> p q (a b) o", q=PH, o=GC),
                                  cbias.rearrange("p (b o) -> p b o", o=GC).unsqueeze(1).to_broadcast([P, PH, NG, GC]),
                                  ALU.add).then_inc(S["cT_ready"], 1)

            def router_max(i):
                dve.wait_ge(S["low_ready"], i - 1)
                dve.tensor_tensor(fs[:, 4:4 + EX], ffn_banks(i)[:, 0, LOW:LOW + EX], brb[:, :], ALU.add
                                  ).then_inc(S["router_sum0"], 1)
                dve.wait_ge(S["router_sum0"], i - 1)
                dve.tensor_reduce(fs[:, 0:1], fs[:, 4:4 + EX], AX, ALU.max, negate=True
                                  ).then_inc(S["router_max"], 1)

            def router(i):
                dve.wait_ge(S["router_exp"], i - 1)
                dve.reciprocal(fs[:, 2:3], fs[:, 1:2]).then_inc(S["router_sum"], 1)
                dve.wait_ge(S["router_sum"], i - 1)
                dve.tensor_scalar(fs[:, 4 + 2 * EX:4 + 3 * EX], fs[:, 4 + EX:4 + 2 * EX], fs[:, 2:3], FFN_SCALE,
                                  ALU.mult, ALU.mult).then_inc(S["router_w"], 1)
                dve.wait_ge(S["router_w"], i - 1)
                dve.tensor_tensor(lows[:, :].rearrange("p (e r) -> p e r", r=R),
                                  ffn_banks(i)[:, 0, 0:LOW].rearrange("p (e r) -> p e r", r=R),
                                  fs[:, 4 + 2 * EX:4 + 3 * EX].unsqueeze(2).to_broadcast([P, EX, R]), ALU.mult
                                  ).then_inc(S["lows_ready"], 1)

            def turn_probs(i, part):
                if part == 0:
                    dve.wait_ge(S["probs0"], i)
                rows = sm[:, 0, :, :].rearrange("p (m h) k -> p m (h k)", h=2)
                for a in range(part * T, (part + 1) * T, 32):
                    for b in range(0, P, 32):
                        ins = dve.transpose(pT[b:b + 32, 0:8, a:a + 32], rows[a:a + 32, :, b:b + 32])
                if part == 1:
                    ins.then_inc(S["pT0_ready"], 1)

            def probs(i, s):
                dve.wait_ge(S[f"pT{s}_turned"], i if s else 1)
                dve.tensor_copy(pT[:, 8 * s + 4:8 * s + 8, :], B[:, 2 * s + 1, :].rearrange("p (m t) -> p m t", m=4)
                                ).then_inc(S[f"pT{s}_ready"], 1)

            def result(i):
                dve.wait_ge(S["f_ready"], i - 1)
                if not (isinstance(i, int) and i == 2):
                    dve.wait_ge(s_out, 16 * (i - 2))
                f = ffn_banks(i).rearrange("p a c -> p (a c)")
                for view in phases:
                    ins = dve.tensor_tensor(view(res), view(f), x1_of(x1_at(i - 1), view, 0, D // PH), ALU.add)
                ins.then_inc(S["result_ready"], 1)

            def low_o(i):
                dve.wait_ge(S["o_high_ready"], i)
                dve.scalar_tensor_tensor(oT[:, 1, :, :], CC.rearrange("p a (c t) -> p (a c) t", c=4), o_s,
                                         oT[:, 0, :, :], ALU.mult, ALU.subtract).then_inc(S["oT_ready"], 1)

            def residual(i, n):
                dve.wait_ge(s_res, 16 * i)
                dve.wait_ge(S["op_ready"], i)
                dve.wait_ge(s_wo[n], i)
                for view in phases:
                    ins = dve.scalar_tensor_tensor(x1_of(x1_at(i), view, n * BLK // PH, BLK // PH), view(A[n]),
                                                   op[:, n:n + 1], view(xres[:, n * BLK:(n + 1) * BLK]), ALU.mult, ALU.add)
                ins.then_inc(S["x1a_ready" if n == 0 else "x1b_ready"], 1)

            def step(i, proj, attn, tail, more):
                first = isinstance(i, int) and i == 0
                second = isinstance(i, int) and i == 1
                if attn and not second:
                    keys(i, 0)
                if proj:
                    rotate(i, 0)
                if second:
                    max_w(7)
                if first:
                    max_w(5)
                    low_w(3)
                    scale_w(5)
                if proj:
                    rotate(i, 1)
                if second:
                    scale_w(7)
                if first:
                    max_w(6)
                    low_w(4)
                    scale_w(6)
                if attn:
                    mask_max(i, 0)
                    keys(i, 1)
                if tail:
                    conv_bias(i)
                if attn:
                    sums(i, 0)
                if proj:
                    rotate(i, 2)
                if first:
                    low_w(5)
                if attn:
                    mask_max(i, 1)
                if tail:
                    router_max(i)
                if attn:
                    turn_probs(i, 0)
                    sums(i, 1)
                if tail:
                    router(i)
                if proj:
                    rotate(i, 3)
                if attn:
                    turn_probs(i, 1)
                if first:
                    mixed(1)
                if attn:
                    probs(i, 1)
                if tail:
                    result(i)
                if second:
                    low_w(7)
                if more and not first:
                    mixed(i + 1)
                if isinstance(i, int) and i == NP - 1:
                    keys(NP, 0)
                    keys(NP, 1)
                if attn:
                    low_o(i)
                if proj:
                    values(i, 0)
                if more:
                    scale_y(i + 1)
                if first:
                    low_y(1)
                    low_w(6)
                if proj:
                    values(i, 1)
                if more and not first:
                    low_y(i + 1)
                if proj and not (isinstance(i, int) and i == NP - 1):
                    max_v(i)
                    if first:
                        keys(1, 0)
                    scale_o(i)
                if attn and not (isinstance(i, int) and i == NP - 1):
                    residual(i, 0)
                    residual(i, 1)

            def finish():
                mask_max(NP, 0)
                mask_max(NP, 1)
                max_v(NP - 1)
                sums(NP, 0)
                sums(NP, 1)
                residual(NP - 1, 0)
                residual(NP - 1, 1)
                scale_o(NP - 1)
                probs(NP, 0)
                probs(NP, 1)
                low_o(NP)
                dve.wait_ge(s_gs, 7)
                residual(NP, 0)
                residual(NP, 1)
                conv_bias(NP)
                router_max(NP)
                router(NP)
                conv_bias(NP + 1)
                result(NP)
                router_max(NP + 1)
                router(NP + 1)
                result(NP + 1)

            steps(dve, step, finish)


LATE_AT = tuple(np.cumsum([0, NG * PW, D, D, GROUPS * SHIFTS * P]).tolist())
LATE = max(LATE_AT[-1], WCOL)
V_ATT, V_ATTT, V_MIX0, V_BIAS = 4, 6, 17, 18
A_CTX, A_MIX = 2, 4
PE_MIX = 8


def kernel(**inputs):
    import numpy as np
    import concourse.bacc as _bacc
    from concourse import mybir as _mybir
    from concourse.bass_utils import run_bass_kernel_spmd as _run

    g = {k: np.asarray(v) for k, v in inputs.items()}

    def c(a):
        return np.ascontiguousarray(a)

    wt = g["L0_cond2_weight"]
    toep = np.zeros((GC, PH, GROUPS, SHIFTS, PH, GC), wt.dtype)
    for gp in range(GROUPS):
        for ph in range(PH):
            for q in range(PH):
                for d in range(SHIFTS):
                    k = PH * d + ph - q
                    if 0 <= k < TAPS:
                        toep[:, ph, gp, d, q, :] = wt[gp * GC:(gp + 1) * GC, :, k].T
    t = np.arange(T, dtype=np.float32)
    pack = np.zeros((P, PACKED), np.float32)
    mixk = g["L0_cond_weight"].reshape(KMIX, T, T)
    for name, a in (("W0", g["L0_cond_W0"]), ("W1", g["L0_cond_W1"]), ("W2", g["L0_cond_W2"]),
                    ("b0", g["L0_cond_b0"][:, None]), ("b1", g["L0_cond_b1"][:, None]),
                    ("cw", g["L0_cond2_c_weight"].T), ("cond", g["cond_128"].T),
                    ("mix", np.tile(mixk.transpose(2, 0, 1).reshape(T, KMIX * T), (2, 1))),
                    ("halves", np.arange(NB)[:, None] == np.arange(P)[None, :] // T), ("bias_k", g["L0_cond_bias_k"]), ("b2", g["L0_cond_b2"][None]), ("fside", g["fside_S_0"][None]),
                    ("br", g["L0_ffn_br"][None])):
        pack[:a.shape[0], PACK[name]] = a
    arrays = {
        "x": c(g["x"].reshape(NB * T, D)),
        "pack": pack,
        "shapes": np.concatenate([
            np.eye(P, dtype=np.float32), np.tile(np.triu(np.full((T, T), NEG, np.float32), 1), (2, 1)),
            np.tile(np.stack([np.cos(t), np.sin(t)], 1), (2, 1)).astype(np.float32)], 1),
        "mixk": c(mixk.transpose(0, 2, 1).reshape(KMIX, T * T)),
        "wqkvoT": c(np.stack([g["L0_attn_wq"].T, g["L0_attn_wk"].T, g["L0_attn_wv"].T, g["L0_attn_wo"].T])),
        "toep": toep.reshape(P, GROUPS, SHIFTS, P),
        "abT": c(np.concatenate([g["L0_ffn_A"].reshape(LOW, D), g["L0_ffn_Wr"]]).T),
        "bmT": c(g["L0_ffn_B"].transpose(0, 2, 1).reshape(LOW, D)),
    }
    nc = _bacc.Bacc("TRN2", target_bir_lowering=False, num_devices=1, dynamic_dma_scratch_size=1024)
    args = {k: nc.dram_tensor(k + "_dram", a.shape, _mybir.dt.from_np(a.dtype), kind="ExternalInput").ap()
            for k, a in arrays.items()}
    out = nc.dram_tensor("out_dram", (NB * T, D), F32, kind="ExternalOutput").ap()
    build(nc, **args, out=out)
    r = _run(nc, [{k + "_dram": a for k, a in arrays.items()}], core_ids=[0])
    return r.results[0]["out_dram"].reshape(NB, T, D)
```
